# Optimizing a Trainium2 kernel written in Bass

```python
import numpy as np
import jax
import jax.numpy as jnp

def _softmax(x, axis=-1):
    return jax.nn.softmax(x, axis=axis)

def _gelu(x):
    return jax.nn.gelu(x, approximate=True)

def _silu(x):
    return jax.nn.silu(x)

def _sigmoid(x):
    return jax.nn.sigmoid(x)

def _layernorm(x, axis=-1, eps=1e-05):
    m = jnp.mean(x, axis=axis, keepdims=True)
    v = jnp.var(x, axis=axis, keepdims=True)
    return (x - m) / jnp.sqrt(v + eps)

def _scatter_add(tgt, idx, src, axis=0):
    return tgt.at[idx].add(src)

def _segment_sum(src, seg, n):
    return jax.ops.segment_sum(src, seg, n)
kernel_name = 'mk_seq_preln_d1_jaxref_r8_823598'

def setup_inputs(seed: int=0):
    np.random.seed(seed)
    _w = jnp.asarray

    def _L0_attn_setup():
        import jax, jax.numpy as jnp
        import numpy as np
        B, S, D = (2, 256, 128)
        N_HEADS, N_KV_HEADS = (16, 4)
        HEAD_DIM = D // N_HEADS
        KV_GROUPS = N_HEADS // N_KV_HEADS
        ROPE_BASE = 10000.0

        def _apply_rope(t, cos, sin):
            t1, t2 = jnp.split(t, 2, axis=-1)
            return jnp.concatenate([t1 * cos - t2 * sin, t1 * sin + t2 * cos], axis=-1)
        key = jax.random.key(seed)
        ks = jax.random.split(key, 5)
        s = 0.02
        return {'x': jax.random.normal(ks[0], (B, S, D), dtype=jnp.float32), 'wq': jax.random.normal(ks[1], (D, D), dtype=jnp.float32) * s, 'wk': jax.random.normal(ks[2], (D, N_KV_HEADS * HEAD_DIM), dtype=jnp.float32) * s, 'wv': jax.random.normal(ks[3], (D, N_KV_HEADS * HEAD_DIM), dtype=jnp.float32) * s, 'wo': jax.random.normal(ks[4], (D, D), dtype=jnp.float32) * s}
    _L0_attn_in = _L0_attn_setup()

    def _L0_ffn_setup():
        import jax, jax.numpy as jnp
        import numpy as np
        B, S, H, E, K, I = (1, 64, 128, 16, 4, 128)
        ALPHA, LIMIT = (1.702, 7.0)
        key = jax.random.key(seed)
        ks = jax.random.split(key, 7)
        return {'hidden_states': jax.random.normal(ks[0], (B, S, H), jnp.float32), 'router_w': jax.random.normal(ks[1], (H, E), jnp.float32) * 0.02, 'router_b': jax.random.normal(ks[2], (E,), jnp.float32) * 0.02, 'gate_up_proj': jax.random.normal(ks[3], (E, H, 2 * I), jnp.float32) * 0.02, 'gate_up_bias': jax.random.normal(ks[4], (E, 2 * I), jnp.float32) * 0.02, 'down_proj': jax.random.normal(ks[5], (E, I, H), jnp.float32) * 0.02, 'down_bias': jax.random.normal(ks[6], (E, H), jnp.float32) * 0.02}
    _L0_ffn_in = _L0_ffn_setup()
    _d = {'L0_attn_x': _L0_attn_in['x'], 'L0_attn_wq': _L0_attn_in['wq'], 'L0_attn_wk': _L0_attn_in['wk'], 'L0_attn_wv': _L0_attn_in['wv'], 'L0_attn_wo': _L0_attn_in['wo'], 'L0_ffn_router_w': _L0_ffn_in['router_w'], 'L0_ffn_router_b': _L0_ffn_in['router_b'], 'L0_ffn_gate_up_proj': _L0_ffn_in['gate_up_proj'], 'L0_ffn_gate_up_bias': _L0_ffn_in['gate_up_bias'], 'L0_ffn_down_proj': _L0_ffn_in['down_proj'], 'L0_ffn_down_bias': _L0_ffn_in['down_bias']}
    _x0 = _d['L0_attn_x']
    _d['L0_attn_x'] = jax.random.normal(jax.random.fold_in(jax.random.key(seed), 1), (8, 512, 128), dtype=_x0.dtype)
    del _x0
    return _d

def reference(L0_attn_x, L0_attn_wq, L0_attn_wk, L0_attn_wv, L0_attn_wo, L0_ffn_router_w, L0_ffn_router_b, L0_ffn_gate_up_proj, L0_ffn_gate_up_bias, L0_ffn_down_proj, L0_ffn_down_bias):

    def _L0_attn_ref(x, wq, wk, wv, wo):
        import jax, jax.numpy as jnp
        import numpy as np
        B, S, D = (2, 256, 128)
        N_HEADS, N_KV_HEADS = (16, 4)
        HEAD_DIM = D // N_HEADS
        KV_GROUPS = N_HEADS // N_KV_HEADS
        ROPE_BASE = 10000.0

        def _apply_rope(t, cos, sin):
            t1, t2 = jnp.split(t, 2, axis=-1)
            return jnp.concatenate([t1 * cos - t2 * sin, t1 * sin + t2 * cos], axis=-1)
        Bx, Sx, Dx = x.shape
        q = (x @ wq).reshape(Bx, Sx, N_HEADS, HEAD_DIM)
        k = (x @ wk).reshape(Bx, Sx, N_KV_HEADS, HEAD_DIM)
        v = (x @ wv).reshape(Bx, Sx, N_KV_HEADS, HEAD_DIM)
        half = HEAD_DIM // 2
        inv_freq = 1.0 / ROPE_BASE ** (jnp.arange(0, half, dtype=jnp.float32) / half)
        pos = jnp.arange(Sx, dtype=jnp.float32)
        ang = pos[:, None] * inv_freq[None, :]
        cos = jnp.cos(ang)[:, None, :]
        sin = jnp.sin(ang)[:, None, :]
        q = _apply_rope(q, cos, sin)
        k = _apply_rope(k, cos, sin)
        k = jnp.broadcast_to(k[:, :, None, :, :], (Bx, Sx, KV_GROUPS, N_KV_HEADS, HEAD_DIM)).reshape(Bx, Sx, N_HEADS, HEAD_DIM)
        v = jnp.broadcast_to(v[:, :, None, :, :], (Bx, Sx, KV_GROUPS, N_KV_HEADS, HEAD_DIM)).reshape(Bx, Sx, N_HEADS, HEAD_DIM)
        scale = 1.0 / jnp.sqrt(jnp.float32(HEAD_DIM))
        scores = jnp.einsum('bshd,bthd->bhst', q, k) * scale
        causal = jnp.tril(jnp.ones((Sx, Sx), dtype=bool))
        scores = jnp.where(causal[None, None, :, :], scores, jnp.float32(-jnp.inf))
        attn = jax.nn.softmax(scores, axis=-1)
        out = jnp.einsum('bhst,bthd->bshd', attn, v).reshape(Bx, Sx, Dx)
        return out @ wo

    def _L0_ffn_ref(hidden_states, router_w, router_b, gate_up_proj, gate_up_bias, down_proj, down_bias):
        import jax, jax.numpy as jnp
        import numpy as np
        B, S, H, E, K, I = (1, 64, 128, 16, 4, 128)
        ALPHA, LIMIT = (1.702, 7.0)
        b, s, h = hidden_states.shape
        x = hidden_states.reshape(-1, h)
        logits = x @ router_w + router_b
        topv, topi = jax.lax.top_k(logits, K)
        topw = jax.nn.softmax(topv, axis=-1)
        one_hot = (topi[..., None] == jnp.arange(E)).astype(topw.dtype)
        scores = jnp.einsum('tk,tke->te', topw, one_hot)
        gu = jnp.einsum('th,ehf->tef', x, gate_up_proj) + gate_up_bias
        gate = jnp.minimum(gu[..., ::2], LIMIT)
        up = jnp.clip(gu[..., 1::2], -LIMIT, LIMIT)
        glu = gate * jax.nn.sigmoid(gate * ALPHA)
        act = (up + 1.0) * glu
        expert_out = jnp.einsum('tei,eih->teh', act, down_proj) + down_bias
        out = jnp.einsum('te,teh->th', scores, expert_out)
        return out.reshape(b, s, h)
    x = L0_attn_x
    x = x + _L0_attn_ref(_layernorm(x, axis=-1), L0_attn_wq, L0_attn_wk, L0_attn_wv, L0_attn_wo)
    x = x + _L0_ffn_ref(_layernorm(x, axis=-1), L0_ffn_router_w, L0_ffn_router_b, L0_ffn_gate_up_proj, L0_ffn_gate_up_bias, L0_ffn_down_proj, L0_ffn_down_bias)
    return x

_drawn_inputs = setup_inputs


def setup_inputs(seed=0):
    import zlib

    import numpy as np

    out = dict(_drawn_inputs(seed))
    spreads = {}
    factors = {'L0_attn_wq': 8.0,
     'L0_attn_wk': 8.0,
     'L0_attn_wv': 8.0,
     'L0_attn_wo': 8.0,
     'L0_ffn_router_w': 3.801,
     'L0_ffn_router_b': 8.0,
     'L0_ffn_gate_up_proj': 4.154,
     'L0_ffn_gate_up_bias': 8.0,
     'L0_ffn_down_proj': 4.079,
     'L0_ffn_down_bias': 5.573}
    for name, (base, spread) in spreads.items():
        noise = np.random.default_rng([zlib.crc32(name.encode()), seed]).standard_normal(out[name].shape)
        drawn = base * np.exp(spread * noise) if base else spread * noise
        out[name] = jnp.asarray(drawn.astype(out[name].dtype))
    for name, factor in factors.items():
        out[name] = (out[name] * factor).astype(out[name].dtype)
    return out
```

```python
from contextlib import ExitStack

import numpy as np

import concourse.bass as bass
from concourse import mybir

ALU = mybir.AluOpType
ACT = mybir.ActivationFunctionType
F32 = mybir.dt.float32
BF16 = mybir.dt.bfloat16
AX_X = mybir.AxisListType.X

P = 128
B, S, D = 8, 512, 128
NH, NKV, HD = 16, 4, 8
E, TOPK, FF = 16, 4, 128
NT = S // P
NG = NH // NKV
EPS = 1e-5
ALPHA, LIMIT = 1.702, 7.0
NEG = -1.0e30
BIG = 3.0e38

Q_PART = (0, 0, 0, 1, 1, 2)
K_PART = (0, 1, 2, 0, 1, 0)
NR = len(Q_PART)
STACK = NR * HD

NU = NG * NT * 2
NV = NG * NT
NM = NG * 11
RING = 8
LAG = 4
M_SLOT0 = 5

JOBS = (("v", "m"), ("oT0", "tail"), ("xT", "p"), ("oT1", "tail"), ("mB", "m_prev"), ("q", "p"), ("oT2", "tail"), ("qr", "p"),
        ("oT3", "tail"), ("k", "p"), ("onT", "tail"), ("kr", "p"), ("y", "tail"), ("x2", "tail"), ("mA", "m"), ("lg", "tail"),
        ("rT", "tail"), ("bias", "tail"))


def stages(n):
    return {"e": 1 <= n <= B, "e_prev": 2 <= n <= B + 1, "m": 0 <= n < B, "m_prev": 1 <= n <= B, "p": n < B - 1, "tail": n >= 2}


def jobs_of(n):
    return [name for name, stage in JOBS if stages(n)[stage]]


class Step:

    def __init__(self, t, par, like):
        self.t, self.par = t, par
        has = stages(like)
        self.e, self.e_prev, self.m, self.m_prev, self.p, self.tail = (has[k] for k in ("e", "e_prev", "m", "m_prev", "p", "tail"))
        self.jobs = jobs_of(like)
        before = sum(len(jobs_of(n)) for n in range(-1, min(like, 2)))
        self.before = before + len(JOBS) * (t - 2) if 2 <= like <= B - 2 else before + sum(len(jobs_of(n)) for n in range(2, like))

    def filled(self, job):
        return self.before + self.jobs.index(job) + 1

    def free(self, job):
        return self.before + self.jobs.index(job)


def m_slot(m):
    return M_SLOT0 + m * NU // NM


def v_slot(n):
    return 2 * n + LAG


def m_unit(m):
    g, k = divmod(m, 11)
    if k == 0:
        return 0, NG * g, 4
    if k < 3:
        return 1, NG * g + 2 * (k - 1), 2
    return (2, NG * g + k - 3, 1) if k < 7 else (3, NG * g + k - 7, 1)


def m_units_of(st, u):
    before = [(m, st.t - 1, 1 - st.par) for m in range(NM) if m_slot(m) == u + NU and st.m_prev]
    return before + [(m, st.t, st.par) for m in range(NM) if m_slot(m) == u and st.m]


def values_of(st, u):
    before = [(n, st.t - 2, st.par) for n in range(NV) if v_slot(n) == u + NU and st.e_prev]
    return before + [(n, st.t - 1, 1 - st.par) for n in range(NV) if v_slot(n) == u and st.e]


def build(nc, x, wq, wk, wv, wo, router_w, router_b, gate_up, gate_up_b, down, down_b, cos_q, sin_q, cos_k, sin_k, out):
    with ExitStack() as ctx:
        def sb(name, shape, dt=F32):
            return ctx.enter_context(nc.sbuf_tensor(name, shape, dt))

        def sem(name):
            return ctx.enter_context(nc.semaphore(name))

        X = sb("X", [P, B * NT, D])
        x2T = sb("x2T", [P, B * S])
        route = sb("route", [P, B * NT, E])
        ident = sb("ident", [P, P])
        ident_bf = sb("ident_bf", [P, P], BF16)
        mask = sb("mask", [P, 4, P], BF16)
        wq_raw, wk_raw = sb("wq_raw", [P, NH * HD]), sb("wk_raw", [P, NKV * HD])
        wq_p, wq_r = sb("wq_p", [P, HD, NH]), sb("wq_r", [P, HD, NH])
        wk_p, wk_r = sb("wk_p", [P, HD, NKV]), sb("wk_r", [P, HD, NKV])
        wv_s, wo_s = sb("wv_s", [P, NKV * HD]), sb("wo_s", [P, D])
        rw_s, rb_s = sb("rw_s", [P, E]), sb("rb_s", [P, E])
        cosq_s, sinq_s = sb("cosq_s", [P, S]), sb("sinq_s", [P, S])
        cosk_s, sink_s = sb("cosk_s", [NKV * HD, S]), sb("sink_s", [NKV * HD, S])
        gu_s = sb("gu_s", [P, E, 2 * FF])
        dn_s = sb("dn_s", [P, E, D])
        dnb_s = sb("dnb_s", [E, D])
        gub_s = sb("gub_s", [P, E, 2])
        gate_b, up_b = sb("gate_b", [P, E]), sb("up_b", [P, E])
        mhalf, limit = sb("mhalf", [P, NT]), sb("limit", [P, 1])
        stats, mv, veps, rstd = sb("stats", [P, NT, 6]), sb("mv", [P, NT, 2]), sb("veps", [P, NT]), sb("rstd", [P, NT])
        xn, xT = sb("xn", [P, NT, D]), sb("xT", [P, S])
        rope_c, rope_s, rope, left = sb("rope_c", [P, S]), sb("rope_s", [P, S]), sb("rope", [P, S]), sb("left", [P, S])
        qparts = sb("qparts", [P, 3, S], BF16)
        kparts = sb("kparts", [NKV * HD, 3, S], BF16)
        Qs = [sb(f"Qs{i}", [P, NH, S], BF16) for i in range(2)]
        Ks = [sb(f"Ks{i}", [P, NKV, S], BF16) for i in range(2)]
        Km = [sb(f"Km{i}", [P, NKV, S], BF16) for i in range(2)]
        Vs = [sb(f"Vs{i}", [P, NT, NKV, 32]) for i in range(2)]
        probs = sb("probs", [P, RING, 2, S])
        negmax = sb("negmax", [P, NT, NH])
        mparts = [sb(f"mparts{i}", [NH // 2, 2, S], BF16) for i in range(2)]
        oT = [sb(f"oT{i}", [P, NG, S]) for i in range(2)]
        rden, on = sb("rden", [P, NT, NH]), sb("on", [P, NT, D])
        onT = sb("onT", [P, S])
        x1 = sb("x1", [P, NT, D])
        stats2, mv2, veps2, rstd2 = sb("stats2", [P, NT, 6]), sb("mv2", [P, NT, 2]), sb("veps2", [P, NT]), sb("rstd2", [P, NT])
        x2n, x2s = sb("x2n", [P, NT, D]), sb("x2s", [P, S])
        lg, top, first4, cut = sb("lg", [P, NT, 24]), sb("top", [P, NT, 8]), sb("first4", [P, NT, 8]), sb("cut", [P, NT, 24])
        ldiff, lexp, chosen, lsum, lrec = (sb(n, [P, NT, k]) for n, k in (("ldiff", E), ("lexp", E), ("chosen", E), ("lsum", 1), ("lrec", 1)))
        wsel, rt = sb("wsel", [P, NT, E]), sb("rt", [P, NT, E])
        rtT = left[0:E, :]

        ps_e = ctx.enter_context(nc.psum_tensor("ps_e", [P, 2, 2, S], F32))
        ps_m = ctx.enter_context(nc.psum_tensor("ps_m", [P, 2, S], F32))
        ps_o = ctx.enter_context(nc.psum_tensor("ps_o", [P, S], F32))
        ps_x = ctx.enter_context(nc.psum_tensor("ps_x", [P, S], F32))

        q_dram = nc.dram_tensor("q_dram", [2, NR, P, S], BF16, kind="Internal").ap()
        k_dram = nc.dram_tensor("k_dram", [2, NR, NKV * HD, S], BF16, kind="Internal").ap()

        x_first, x_rest, w_in, moe_in, const_rdy = sem("x_first"), sem("x_rest"), sem("w_in"), sem("moe_in"), sem("const_rdy")
        init, perm, zero_v, biases = sem("init"), sem("perm"), sem("zero_v"), sem("biases")
        zero_g = sem("zero_g")
        st_done, mv_done, ve_done, rs_done, xn_done = (sem(n) for n in ("st_done", "mv_done", "ve_done", "rs_done", "xn_done"))
        x_fill, x_read = sem("x_fill"), sem("x_read")
        rope_add = sem("rope_add")
        part_a, part_r, part_b, part_c = sem("part_a"), sem("part_r"), sem("part_b"), sem("part_c")
        q_spill, k_spill = sem("q_spill"), sem("k_spill")
        stack_in = sem("stack_in")
        mx_mm, mx_red = sem("mx_mm"), sem("mx_red")
        mh_done, ml_done, m_in = sem("mh_done"), sem("ml_done"), sem("m_in")
        sc_mm, exp_done, causal = sem("sc_mm"), sem("exp_done"), sem("causal")
        pv_mm, o_ev = sem("pv_mm"), sem("o_ev")
        rden_done = sem("rden_done")
        st2_done, mv2_done, ve2_done, rs2_done, x2n_done = (sem(n) for n in ("st2_done", "mv2_done", "ve2_done", "rs2_done", "x2n_done"))
        x2_kept, top_done, first_done, diff_done, lexp_done = (sem(n) for n in ("x2_kept", "top_done", "first_done", "diff_done", "lexp_done"))
        cut_done, chosen_done, wsel_done, lsum_done, lrec_done, rt_done, rt_kept = (
            sem(n) for n in ("cut_done", "chosen_done", "wsel_done", "lsum_done", "lrec_done", "rt_done", "rt_kept"))

        def wait(eng, s, value):
            if not isinstance(value, int) or value > 0:
                eng.wait_ge(s, value)

        def tiles(t):
            return bass.ds(t * NT, NT)

        def steps(eng, step):
            for t in (-1, 0, 1):
                step(Step(t, t % 2, t))
            with eng.Fori(2, 5, 2) as t:
                step(Step(t, 0, 2))
                step(Step(t + 1, 1, 3))
            for t in range(B - 2, B + 2):
                step(Step(t, t % 2, t))

        gate_mm, up_mm = sem("gate_mm"), sem("up_mm")
        relu_done, v_done, act_done, down_mm, acc_done = (sem(n) for n in ("relu_done", "v_done", "act_done", "down_mm", "acc_done"))
        glu_done, rc_done, out_done = sem("glu_done"), sem("rc_done"), sem("out_done")
        rc, acc = sb("rc", [P, NT, E]), x1

        def ps_gate(e):
            return ps_e[:, e % 2, 0, :]

        def ps_up(e):
            return ps_e[:, e % 2, 1, :]

        def ps_down(e):
            return ps_m[:, e % 2, :]

        def relu_s(e):
            return probs[:, e % 2, 0, :]

        def glu_s(e):
            return probs[:, e % 2, 1, :]

        def v_s(e):
            return probs[:, 2 + e % 2, 0, :]

        def act_s(e):
            return probs[:, 4 + e % 2, 0, :]

        def pe_experts(pe):
            mm = nc.tensor.matmul
            pe.sem_inc(down_mm, 2)
            pe.wait_ge(x2_kept, B)
            pe.wait_ge(exp_done, NU * B)

            def down(c, e):
                pe.wait_ge(act_done, E * c + e + 3)
                pe.wait_ge(acc_done, E * c + e + 1)
                for i in range(NT):
                    last = mm(ps_down(e)[:, D * i:D * (i + 1)], act_s(e)[:, P * i:P * (i + 1)], dn_s[:, e, :], start=True, stop=True)
                last.then_inc(down_mm, 1)

            with pe.Fori(0, B) as c:
                for e in range(E):
                    x2 = x2T[:, bass.ds(c * S, S)]
                    pe.wait_ge(relu_done, E * c + e + 1)
                    mm(ps_gate(e), gu_s[:, e, 0:2 * FF:2], x2, start=True, stop=True).then_inc(gate_mm, 1)
                    pe.wait_ge(v_done, E * c + e + 1)
                    mm(ps_up(e), gu_s[:, e, 1:2 * FF:2], x2, start=True, stop=True).then_inc(up_mm, 1)
                    if e:
                        down(c, e - 1)
                down(c, E - 1)

        def act_experts(act):
            act.sem_inc(relu_done, 2)
            act.wait_ge(biases, 2)
            act.wait_ge(const_rdy, 4)
            with act.Fori(0, B) as c:
                for e in range(E):
                    act.wait_ge(gate_mm, E * c + e + 1)
                    nc.scalar.activation(relu_s(e), ps_gate(e), ACT.Relu, bias=gate_b[:, e:e + 1], scale=-1.0).then_inc(relu_done, 1)
                    act.wait_ge(relu_done, E * c + e + 3)
                    act.wait_ge(act_done, E * c + e + 1)
                    nc.scalar.activation(glu_s(e), relu_s(e), ACT.Gelu_apprx_sigmoid, bias=limit[:], scale=-1.0).then_inc(glu_done, 1)

        def dve_experts(dve):
            v = nc.vector
            dve.sem_inc(v_done, 2)
            dve.sem_inc(act_done, 2)
            dve.sem_inc(acc_done, 2)
            dve.wait_ge(rt_kept, B)

            def accumulate(c, e):
                dve.wait_ge(down_mm, E * c + e + 3)
                dve.wait_ge(acc_done, E * c + e + 2)
                for i in range(NT):
                    here = X[:, bass.ds(c * NT + i, 1), :].rearrange("p a d -> p (a d)")
                    last = v.scalar_tensor_tensor(out=here if e == E - 1 else acc[:, i, :], in0=ps_down(e)[:, D * i:D * (i + 1)],
                                                  scalar=rc[:, i, e:e + 1], in1=here if e == 0 else acc[:, i, :],
                                                  op0=ALU.mult, op1=ALU.add)
                last.then_inc(acc_done, 1)

            with dve.Fori(0, B) as c:
                dve.wait_ge(acc_done, E * c + 2)
                v.tensor_copy(rc[:], route[:, tiles(c), :]).then_inc(rc_done, 1)
                dve.wait_ge(rc_done, c + 1)
                for e in range(E):
                    dve.wait_ge(up_mm, E * c + e + 1)
                    v.tensor_scalar(v_s(e), ps_up(e), up_b[:, e:e + 1], LIMIT + 1.0, ALU.add, ALU.min).then_inc(v_done, 1)
                    dve.wait_ge(glu_done, E * c + e + 1)
                    dve.wait_ge(v_done, E * c + e + 3)
                    dve.wait_ge(down_mm, E * c + e + 1)
                    v.scalar_tensor_tensor(out=act_s(e), in0=v_s(e), scalar=1.0 - LIMIT, in1=glu_s(e),
                                           op0=ALU.max, op1=ALU.mult).then_inc(act_done, 1)
                    if e:
                        accumulate(c, e - 1)
                accumulate(c, E - 1)

        block = ctx.enter_context(nc.Block())

        @block.sync
        def _(sp):
            sp.dma_start(X[:, 0:NT, :], x[0].rearrange("(i p) d -> p i d", p=P)).then_inc(x_first, 16)
            sp.dma_start(wq_raw[:], wq).then_inc(w_in, 16)
            sp.dma_start(wk_raw[:], wk).then_inc(w_in, 16)
            sp.dma_start(wv_s[:], wv).then_inc(w_in, 16)
            sp.dma_start(cosq_s[:], cos_q).then_inc(w_in, 16)
            sp.dma_start(sinq_s[:], sin_q).then_inc(w_in, 16)
            sp.dma_start(cosk_s[:], cos_k).then_inc(w_in, 16)
            sp.dma_start(sink_s[:], sin_k).then_inc(w_in, 16)
            sp.dma_start(wo_s[:], wo).then_inc(w_in, 16)
            sp.dma_start(X[:, NT:B * NT, :], x[1:B].rearrange("b (i p) d -> p (b i) d", p=P)).then_inc(x_rest, 16)
            sp.dma_start(rw_s[:], router_w).then_inc(moe_in, 16)
            sp.dma_start(rb_s[:], router_b.unsqueeze(0).to_broadcast([P, E])).then_inc(moe_in, 16)
            sp.dma_start(dnb_s[:], down_b).then_inc(moe_in, 16)
            sp.dma_start(gub_s[:], gate_up_b.rearrange("e (f two) -> f e two", two=2)).then_inc(moe_in, 16)
            sp.dma_start(gu_s[:], gate_up.rearrange("e h f -> h e f")).then_inc(moe_in, 16)
            sp.dma_start(dn_s[:], down.rearrange("e f h -> f e h")).then_inc(moe_in, 16)
            sp.wait_ge(zero_v, 6)
            sp.wait_ge(zero_g, 8)

            def load_max(batch, par, half):
                sp.wait_ge(ml_done, 2 * batch + half + 1)
                heads = slice(8 * half, 8 * half + 8)
                sp.dma_start(Qs[par][STACK:STACK + 1, heads, :], mparts[half][:, 0, :]).then_inc(m_in, 16)
                sp.dma_start(Qs[par][STACK + 1:STACK + 2, heads, :], mparts[half][:, 1, :]).then_inc(m_in, 16)

            def step(st):
                t, par, nxt = st.t, st.par, 1 - st.par
                if st.m_prev:
                    load_max(t - 1, 1 - par, 1)
                if st.p:
                    sp.wait_ge(part_c, 2 * (t + 1) + 1)
                    for r in range(NR):
                        sp.dma_start(q_dram[nxt, r], qparts[:, Q_PART[r], :]).then_inc(q_spill, 16)
                    sp.wait_ge(part_c, 2 * (t + 1) + 2)
                    for r in range(NR):
                        sp.dma_start(k_dram[nxt, r], kparts[:, K_PART[r], :]).then_inc(k_spill, 16)
                if st.m:
                    load_max(t, par, 0)
                if st.p:
                    wait(sp, mx_mm, NM * t)
                    sp.wait_ge(k_spill, 96 * (t + 2))
                    k_flat = k_dram[nxt].rearrange("r (d h) t -> (r d) h t", d=HD)
                    sp.dma_start(Km[nxt][0:STACK], k_flat).then_inc(stack_in, 16)
                    wait(sp, sc_mm, NU * t)
                    sp.wait_ge(q_spill, 96 * (t + 2))
                    q_flat = q_dram[nxt].rearrange("r (d h) t -> (r d) h t", d=HD)
                    sp.dma_start(Qs[nxt][0:STACK], q_flat).then_inc(stack_in, 16)
                    sp.dma_start(Ks[nxt][0:STACK], k_flat).then_inc(stack_in, 16)

            steps(sp, step)
            with sp.Fori(0, B) as c:
                sp.wait_ge(acc_done, E * c + E + 2)
                sp.dma_start(out[bass.ds(c, 1)].rearrange("a (i p) d -> p (a i) d", p=P), X[:, tiles(c), :]).then_inc(out_done, 16)
            sp.wait_ge(out_done, 16 * B)

        @block.gpsimd
        def _(pool):
            g = nc.gpsimd
            g.memset(mhalf[:], -0.5).then_inc(const_rdy, 1)
            g.memset(limit[:], LIMIT).then_inc(const_rdy, 1)
            g.memset(ident[:], 0.0).then_inc(init, 1)
            g.memset(mask[:], 0.0).then_inc(init, 1)
            pool.wait_ge(init, 2)
            g.affine_select(out=ident[:], in_=ident[:], compare_op=ALU.not_equal, fill=1.0, base=0,
                            pattern=[[-1, P]], channel_multiplier=1).then_inc(init, 1)
            g.affine_select(out=mask[:], in_=mask[:], compare_op=ALU.is_ge, fill=NEG, base=0,
                            pattern=[[0, 4], [-1, P]], channel_multiplier=1).then_inc(const_rdy, 1)
            pool.wait_ge(init, 3)
            g.tensor_copy(ident_bf[:], ident[:]).then_inc(const_rdy, 1)

            g.memset(Qs[1][:].bitcast(F32), 0.0).then_inc(zero_g, 1)
            g.memset(Km[1][:].bitcast(F32), 0.0).then_inc(zero_g, 1)
            g.memset(Ks[1][:].bitcast(F32), 0.0).then_inc(zero_g, 1)
            g.memset(Vs[1][:], 0.0).then_inc(zero_g, 1)
            g.memset(lg[:], BIG).then_inc(zero_g, 1)
            g.memset(first4[:], BIG).then_inc(zero_g, 1)
            pool.wait_ge(zero_g, 6)
            g.memset(Vs[1][:, :, :, HD:HD + 1], 1.0).then_inc(zero_g, 1)
            pool.wait_ge(zero_g, 7)
            g.memset(Ks[1][32:64], 1.0).then_inc(zero_g, 1)
            pool.wait_ge(zero_g, 8)

            def step(st):
                t = st.t
                for u in range(NU):
                    if st.e:
                        pool.wait_ge(exp_done, NU * (t - 1) + u + 1)
                        pool.nop(nofuse=True)
                        diag = probs[:, u % RING, :, 0:P]
                        g.affine_select(out=diag, in_=diag, compare_op=ALU.is_ge, fill=0.0, base=0,
                                        pattern=[[0, 2], [1, P]], channel_multiplier=-1).then_inc(causal, 1)
                    if st.p and u == 1:
                        pool.wait_ge(ve_done, t + 2)
                        g.tensor_tensor(rstd[:], veps[:], mhalf[:], ALU.pow).then_inc(rs_done, 1)
                    if st.p and u == 9:
                        pool.wait_ge(x_read, st.filled("qr"))
                        g.tensor_tensor(rope[:], rope_c[:], rope_s[:], ALU.add).then_inc(rope_add, 1)
                    if st.p and u == 14:
                        pool.wait_ge(x_read, st.filled("kr"))
                        pool.wait_ge(part_r, 2 * (t + 1) + 1)
                        g.tensor_tensor(rope[0:32], rope_c[0:32], rope_s[0:32], ALU.add).then_inc(rope_add, 1)
                    if st.tail and u == 16:
                        pool.wait_ge(ve2_done, t - 1)
                        g.tensor_tensor(rstd2[:], veps2[:], mhalf[:], ALU.pow).then_inc(rs2_done, 1)
                    if st.tail and u == 21:
                        pool.wait_ge(x_read, st.filled("x2"))
                        g.tensor_copy(x2T[:, bass.ds((t - 2) * S, S)], x2s[:]).then_inc(x2_kept, 1)
                    if st.tail and u == 28:
                        pool.wait_ge(rt_done, t - 1)
                        g.tensor_copy(route[:, tiles(t - 2), :], rt[:]).then_inc(rt_kept, 1)

            steps(pool, step)

        @block.tensor
        def _(pe):
            mm = nc.tensor.matmul
            pe.wait_ge(const_rdy, 4)
            pe.wait_ge(perm, 6)

            def turn(job, st, source, rows=P):
                pe.wait_ge(x_read, st.free(job))
                for i in range(NT):
                    last = nc.tensor.transpose(ps_x[0:rows, P * i:P * (i + 1)], source(i), ident[:])
                last.then_inc(x_fill, 1)

            def product(job, st, left_side, right_side, width):
                pe.wait_ge(x_read, st.free(job))
                for i in range(NT):
                    last = mm(ps_x[:, width * i:width * (i + 1)], left_side[:, P * i:P * (i + 1)], right_side[:], start=True, stop=True)
                last.then_inc(x_fill, 1)

            def project(job, st, rows, w):
                pe.wait_ge(x_read, st.free(job))
                mm(ps_x[0:rows], w[:], xT[:], start=True, stop=True).then_inc(x_fill, 1)

            def step(st):
                t, par = st.t, st.par
                if isinstance(t, int) and t == 1:
                    pe.wait_ge(moe_in, 16 * 6)
                for u in range(NU):
                    if st.e:
                        g, j, pair = u // 8, u // 2 % NT, u % 2
                        if u in (0, NU // 2):
                            pe.wait_ge(m_in, 64 * (t - 1) + (32 if u == 0 else 64))
                        wait(pe, exp_done, NU * (t - 1) + u - 1)
                        for k in range(2):
                            h = NG * g + 2 * pair + k
                            last = mm(ps_e[:, u % 2, k, 0:S - P * j], Ks[1 - par][:, h % NKV, P * j:P * (j + 1)],
                                      Qs[1 - par][:, h, P * j:S], start=True, stop=True)
                        last.then_inc(sc_mm, 1)
                    for n, batch, bpar in values_of(st, u):
                        g, j = n // NT, n % NT
                        if j == 0:
                            wait(pe, o_ev, NG * batch + g)
                        pe.wait_ge(causal, NU * batch + 2 * n + 2)
                        for k in range(4):
                            last = mm(ps_o[32 * k:32 * k + 32, P * j:S], Vs[bpar][:, j, k, :],
                                      probs[:, (2 * n + k // 2) % RING, k % 2, 0:S - P * j],
                                      start=(j == 0), stop=(j == NT - 1))
                        last.then_inc(pv_mm, 1)
                    if st.m and u == 2:
                        pe.wait_ge(x_read, st.free("v"))
                        for i in range(NT):
                            last = mm(ps_x[:, 32 * i:32 * i + 32], xT[:, P * i:P * (i + 1)], wv_s[:], start=True, stop=True)
                        last.then_inc(x_fill, 1)
                    if st.tail and u in (3, 5, 8, 10):
                        i = (3, 5, 8, 10).index(u)
                        pe.wait_ge(o_ev, NG * (t - 1))
                        turn(f"oT{i}", st, lambda g: oT[par][:, g, P * i:P * (i + 1)])
                    if st.p and u == 4:
                        pe.wait_ge(xn_done, t + 2)
                        turn("xT", st, lambda i: xn[:, i, :])
                    if st.m_prev and u == 6:
                        pe.wait_ge(mx_red, NM * t)
                        turn("mB", st, lambda i: negmax[:, i, 8:16], rows=8)
                    if st.p and u == 7:
                        pe.wait_ge(x_read, st.filled("xT"))
                        project("q", st, P, wq_p)
                    if st.p and u == 9:
                        project("qr", st, P, wq_r)
                    if st.p and u == 11:
                        project("k", st, 32, wk_p)
                    if st.tail and u == 12:
                        pe.wait_ge(x_read, st.filled("oT3"))
                        turn("onT", st, lambda i: on[:, i, :])
                    if st.p and u == 13:
                        project("kr", st, 32, wk_r)
                    if st.tail and u == 14:
                        pe.wait_ge(x_read, st.filled("onT"))
                        product("y", st, onT, wo_s, D)
                    if st.tail and u == 20:
                        pe.wait_ge(x2n_done, t - 1)
                        turn("x2", st, lambda i: x2n[:, i, :])
                    if st.m and u == 22:
                        pe.wait_ge(mx_red, NM * t + NM // 2)
                        turn("mA", st, lambda i: negmax[:, i, 0:8], rows=8)
                    if st.tail and u == 23:
                        pe.wait_ge(x_read, st.filled("x2"))
                        product("lg", st, x2s, rw_s, E)
                    if st.tail and u == 28:
                        pe.wait_ge(rt_done, t - 1)
                        turn("rT", st, lambda i: rt[:, i, :], rows=E)
                    if st.tail and u == 30:
                        pe.wait_ge(x_read, st.filled("rT"))
                        product("bias", st, rtT, dnb_s, D)
                    for m, batch, bpar in m_units_of(st, u):
                        i, h0, nh = m_unit(m)
                        w = P * (i + 1)
                        if m == 0:
                            pe.wait_ge(stack_in, 48 * (batch + 1))
                        wait(pe, mx_red, NM * batch + m - 1)
                        bank = ps_m[:, m % 2, 0:nh * w].rearrange("p (h k) -> p h k", h=nh)
                        mm(bank[:, :, P * i:w], ident_bf[:], mask[:, 0:nh, :], start=True, stop=False, skip_group_check=True)
                        for k in range(nh):
                            h = h0 + k
                            last = mm(bank[:, k, :], Qs[bpar][:, h, P * i:w], Km[bpar][:, h % NKV, 0:w],
                                      start=False, stop=True, skip_group_check=True)
                        last.then_inc(mx_mm, 1)

            steps(pe, step)
            pe_experts(pe)

        @block.scalar
        def _(act):
            a = nc.scalar

            def step(st):
                t, par = st.t, st.par
                for u in range(NU):
                    if st.e:
                        j = u // 2 % NT
                        wait(act, pv_mm, NV * (t - 1) + (u - RING) // 2 + 1)
                        act.wait_ge(sc_mm, NU * (t - 1) + u + 1)
                        a.activation(probs[:, u % RING, :, 0:S - P * j], ps_e[:, u % 2, :, 0:S - P * j],
                                     ACT.Exp).then_inc(exp_done, 1)
                    for n, batch, bpar in values_of(st, u):
                        if n % NT == NT - 1:
                            g = n // NT
                            act.wait_ge(pv_mm, NV * batch + n + 1)
                            a.activation(oT[bpar][:, g, :], ps_o[:], ACT.Copy).then_inc(o_ev, 1)
                    if st.m and u == 2:
                        if isinstance(t, int) and t == 0:
                            act.wait_ge(zero_v, 6)
                            act.wait_ge(zero_g, 8)
                        wait(act, pv_mm, NV * (t - 1))
                        act.wait_ge(x_fill, st.filled("v"))
                        a.activation(Vs[par][:, :, :, 0:HD], ps_x[:, 0:NT * 32].rearrange("p (i k d) -> p i k d", i=NT, d=HD),
                                     ACT.Copy).then_inc(x_read, 1)
                    if st.p and u == 4:
                        act.wait_ge(x_fill, st.filled("xT"))
                        a.activation(xT[:], ps_x[:], ACT.Copy).then_inc(x_read, 1)
                    if st.p and u in (11, 16):
                        w, parts, n = (P, qparts, 1) if u == 11 else (32, kparts, 2)
                        wait(act, q_spill if u == 11 else k_spill, 96 * (t + 1))
                        act.wait_ge(rope_add, 2 * (t + 1) + n)
                        a.activation(parts[:, 0, :], rope[0:w], ACT.Copy).then_inc(part_a, 1)
                    if st.p and u in (13, 18):
                        w, parts, n = (P, qparts, 1) if u == 13 else (32, kparts, 2)
                        act.wait_ge(part_r, 2 * (t + 1) + n)
                        a.activation(parts[:, 1, :], left[0:w], ACT.Copy).then_inc(part_b, 1)
                    if st.tail and u == 12:
                        act.wait_ge(x_fill, st.filled("onT"))
                        a.activation(onT[:], ps_x[:], ACT.Copy).then_inc(x_read, 1)
                    if st.tail and u == 20:
                        act.wait_ge(x_fill, st.filled("x2"))
                        wait(act, x2_kept, t - 2)
                        a.activation(x2s[:], ps_x[:], ACT.Copy).then_inc(x_read, 1)
                    if st.tail and u == 25:
                        act.wait_ge(diff_done, t - 1)
                        a.activation(lexp[:], ldiff[:], ACT.Exp).then_inc(lexp_done, 1)
                    if st.tail and u == 28:
                        act.wait_ge(x_fill, st.filled("rT"))
                        a.activation(rtT[:], ps_x[0:E, :], ACT.Copy).then_inc(x_read, 1)

            steps(act, step)
            act_experts(act)

        @block.vector
        def _(dve):
            v = nc.vector
            v.memset(Qs[0][:].bitcast(F32), 0.0).then_inc(zero_v, 1)
            v.memset(Km[0][:].bitcast(F32), 0.0).then_inc(zero_v, 1)
            v.memset(Ks[0][:].bitcast(F32), 0.0).then_inc(zero_v, 1)
            v.memset(Vs[0][:], 0.0).then_inc(zero_v, 1)
            dve.wait_ge(zero_v, 4)
            v.memset(Ks[0][32:64], 1.0).then_inc(zero_v, 1)
            v.memset(Vs[0][:, :, :, HD:HD + 1], 1.0).then_inc(zero_v, 1)
            dve.wait_ge(w_in, 16 * 8)
            half = HD // 2
            for raw, plain, swapped, n in ((wq_raw, wq_p, wq_r, NH), (wk_raw, wk_p, wk_r, NKV)):
                cols = raw[:].rearrange("p (h d) -> p d h", d=HD)
                v.tensor_copy(plain[:], cols).then_inc(perm, 1)
                v.tensor_copy(swapped[:, 0:half, :], cols[:, half:HD, :]).then_inc(perm, 1)
                v.tensor_copy(swapped[:, half:HD, :], cols[:, 0:half, :]).then_inc(perm, 1)
            dve.wait_ge(x_first, 16)

            def step(st):
                t, par = st.t, st.par
                if isinstance(t, int) and t == 1:
                    dve.wait_ge(moe_in, 16 * 6)
                    v.tensor_scalar(gate_b[:], gub_s[:, :, 0], -1.0, LIMIT, ALU.mult, ALU.add).then_inc(biases, 1)
                    v.tensor_scalar(up_b[:], gub_s[:, :, 1], 1.0, None, ALU.add).then_inc(biases, 1)
                    dve.wait_ge(zero_g, 8)
                for u in range(NU):
                    if st.p and u == 0:
                        if isinstance(t, int) and t == 0:
                            dve.wait_ge(x_rest, 16)
                        for i in range(NT):
                            last = v.bn_stats(stats[:, i, :], X[:, bass.ds((t + 1) * NT + i, 1), :].rearrange("p a d -> p (a d)"))
                        last.then_inc(st_done, 1)
                        dve.wait_ge(st_done, t + 2)
                        dve.nop(nofuse=True)
                        for i in range(NT):
                            last = v.bn_aggr(mv[:, i, :], stats[:, i, :])
                        last.then_inc(mv_done, 1)
                        dve.wait_ge(mv_done, t + 2)
                        v.tensor_scalar(veps[:], mv[:, :, 1], EPS, None, ALU.add).then_inc(ve_done, 1)
                    if st.p and u == 3:
                        dve.wait_ge(rs_done, t + 2)
                        for i in range(NT):
                            src = X[:, bass.ds((t + 1) * NT + i, 1), :].rearrange("p a d -> p (a d)")
                            last = v.tensor_scalar(xn[:, i, :], src, mv[:, i, 0:1], rstd[:, i:i + 1], ALU.subtract, ALU.mult)
                        last.then_inc(xn_done, 1)
                    if st.tail and u in (3, 5, 8, 10):
                        i = (3, 5, 8, 10).index(u)
                        dve.wait_ge(x_fill, st.filled(f"oT{i}"))
                        heads = ps_x[:].rearrange("p (h w) -> p h w", w=32)
                        v.reciprocal(rden[:, i, :], heads[:, :, HD]).then_inc(rden_done, 1)
                        dve.wait_ge(rden_done, NT * (t - 2) + i + 1)
                        v.tensor_tensor(on[:, i, :].rearrange("p (h d) -> p h d", d=HD), heads[:, :, 0:HD],
                                        rden[:, i, :].unsqueeze(2).to_broadcast([P, NH, HD]), ALU.mult).then_inc(x_read, 1)
                    for job, slot, batch, half in (("mB", 6, t - 1, 1), ("mA", 22, t, 0)):
                        if u == slot and job in st.jobs:
                            dve.wait_ge(x_fill, st.filled(job))
                            wait(dve, m_in, 64 * batch + 32 * half)
                            v.tensor_copy(mparts[half][:, 0, :], ps_x[0:8, :]).then_inc(mh_done, 1)
                            dve.wait_ge(mh_done, 2 * batch + half + 1)
                            v.tensor_tensor(mparts[half][:, 1, :], ps_x[0:8, :], mparts[half][:, 0, :], ALU.subtract).then_inc(ml_done, 1)
                            dve.wait_ge(ml_done, 2 * batch + half + 1)
                            dve.sem_inc(x_read, 1)
                    if st.p and u in (7, 9, 11, 13):
                        job, w, table, to = {7: ("q", P, cosq_s, rope_c), 9: ("qr", P, sinq_s, rope_s),
                                             11: ("k", 32, cosk_s, rope_c), 13: ("kr", 32, sink_s, rope_s)}[u]
                        if u == 11:
                            dve.wait_ge(rope_add, 2 * (t + 1) + 1)
                        dve.wait_ge(x_fill, st.filled(job))
                        v.tensor_tensor(to[0:w], ps_x[0:w], table[:], ALU.mult).then_inc(x_read, 1)
                    if st.p and u in (12, 17):
                        w, parts, n = (P, qparts, 1) if u == 12 else (32, kparts, 2)
                        if u == 17:
                            dve.wait_ge(part_c, 2 * (t + 1) + 1)
                        dve.wait_ge(part_a, 2 * (t + 1) + n)
                        v.tensor_tensor(left[0:w], rope[0:w], parts[:, 0, :], ALU.subtract).then_inc(part_r, 1)
                    if st.p and u in (15, 19):
                        w, parts, n = (P, qparts, 1) if u == 15 else (32, kparts, 2)
                        dve.wait_ge(part_b, 2 * (t + 1) + n)
                        v.tensor_tensor(parts[:, 2, :], left[0:w], parts[:, 1, :], ALU.subtract).then_inc(part_c, 1)
                    if st.tail and u == 14:
                        dve.wait_ge(x_fill, st.filled("y"))
                        v.tensor_tensor(x1[:], X[:, tiles(t - 2), :], ps_x[:].rearrange("p (i d) -> p i d", d=D), ALU.add).then_inc(x_read, 1)
                    if st.tail and u == 15:
                        dve.wait_ge(x_read, st.filled("y"))
                        for i in range(NT):
                            last = v.bn_stats(stats2[:, i, :], x1[:, i, :])
                        last.then_inc(st2_done, 1)
                        dve.wait_ge(st2_done, t - 1)
                        dve.nop(nofuse=True)
                        for i in range(NT):
                            last = v.bn_aggr(mv2[:, i, :], stats2[:, i, :])
                        last.then_inc(mv2_done, 1)
                        dve.wait_ge(mv2_done, t - 1)
                        v.tensor_scalar(veps2[:], mv2[:, :, 1], EPS, None, ALU.add).then_inc(ve2_done, 1)
                    if st.tail and u == 18:
                        dve.wait_ge(rs2_done, t - 1)
                        for i in range(NT):
                            last = v.tensor_scalar(x2n[:, i, :], x1[:, i, :], mv2[:, i, 0:1], rstd2[:, i:i + 1], ALU.subtract, ALU.mult)
                        last.then_inc(x2n_done, 1)
                    if st.tail and u == 23:
                        dve.wait_ge(x_fill, st.filled("lg"))
                        v.tensor_tensor(lg[:, :, 0:E], ps_x[:, 0:NT * E].rearrange("p (i e) -> p i e", e=E),
                                        rb_s[:].unsqueeze(1).to_broadcast([P, NT, E]), ALU.add).then_inc(x_read, 1)
                    if st.tail and u == 24:
                        dve.wait_ge(x_read, st.filled("lg"))
                        dve.nop(nofuse=True)
                        for i in range(NT):
                            last = v.max(top[:, i, :], lg[:, i, 0:E])
                        last.then_inc(top_done, 1)
                        dve.wait_ge(top_done, t - 1)
                        v.tensor_tensor(ldiff[:], lg[:, :, 0:E], top[:, :, 0:1].to_broadcast([P, NT, E]), ALU.subtract).then_inc(diff_done, 1)
                        v.tensor_copy(first4[:, :, 0:TOPK], top[:, :, 0:TOPK]).then_inc(first_done, 1)
                    if st.tail and u == 25:
                        dve.wait_ge(first_done, t - 1)
                        dve.nop(nofuse=True)
                        for i in range(NT):
                            last = v.match_replace(cut[:, i, :], first4[:, i, :], lg[:, i, :], -BIG)
                        last.then_inc(cut_done, 1)
                        dve.wait_ge(cut_done, t - 1)
                        v.tensor_tensor(chosen[:], cut[:, :, 0:E], lg[:, :, 0:E], ALU.not_equal).then_inc(chosen_done, 1)
                    if st.tail and u == 26:
                        dve.wait_ge(chosen_done, t - 1)
                        dve.wait_ge(lexp_done, t - 1)
                        v.tensor_tensor(wsel[:], lexp[:], chosen[:], ALU.mult).then_inc(wsel_done, 1)
                        dve.wait_ge(wsel_done, t - 1)
                        v.tensor_reduce(lsum[:], wsel[:], AX_X, ALU.add).then_inc(lsum_done, 1)
                    if st.tail and u == 27:
                        dve.wait_ge(lsum_done, t - 1)
                        v.reciprocal(lrec[:], lsum[:]).then_inc(lrec_done, 1)
                        dve.wait_ge(lrec_done, t - 1)
                        wait(dve, rt_kept, t - 2)
                        v.tensor_tensor(rt[:], wsel[:], lrec[:].to_broadcast([P, NT, E]), ALU.mult).then_inc(rt_done, 1)
                    if st.tail and u == 30:
                        dve.wait_ge(x_fill, st.filled("bias"))
                        v.tensor_tensor(X[:, tiles(t - 2), :], x1[:], ps_x[:].rearrange("p (i d) -> p i d", d=D), ALU.add).then_inc(x_read, 1)
                    for m, batch, bpar in m_units_of(st, u):
                        i, h0, nh = m_unit(m)
                        w = P * (i + 1)
                        dve.wait_ge(mx_mm, NM * batch + m + 1)
                        v.tensor_reduce(negmax[:, i, h0:h0 + nh], ps_m[:, m % 2, 0:nh * w].rearrange("p (h k) -> p h k", h=nh),
                                        AX_X, ALU.max, negate=True).then_inc(mx_red, 1)

            steps(dve, step)
            dve_experts(dve)


def rope_tables(heads, scale):
    half = HD // 2
    freq = (np.float32(1.0) / np.float32(10000.0) ** (np.arange(half, dtype=np.float32) / np.float32(half))).astype(np.float32)
    ang = np.arange(S, dtype=np.float32)[:, None] * freq[None, :]
    cos = np.concatenate([np.cos(ang), np.cos(ang)], 1).T * np.float32(scale)
    sin = np.concatenate([-np.sin(ang), np.sin(ang)], 1).T * np.float32(scale)
    return tuple(np.ascontiguousarray(np.repeat(t, heads, 0), dtype=np.float32) for t in (cos, sin))


_INS = ["L0_attn_x", "L0_attn_wq", "L0_attn_wk", "L0_attn_wv", "L0_attn_wo", "L0_ffn_router_w", "L0_ffn_router_b",
        "L0_ffn_gate_up_proj", "L0_ffn_gate_up_bias", "L0_ffn_down_proj", "L0_ffn_down_bias"]


def kernel(**inputs):
    import concourse.bacc as bacc
    from concourse.bass_utils import run_bass_kernel_spmd

    nc = bacc.Bacc("TRN2", target_bir_lowering=False, num_devices=1)
    arrays = {f"in_{name}": np.ascontiguousarray(inputs[name]) for name in _INS}
    for name, table in zip(("cos_q", "sin_q", "cos_k", "sin_k"), rope_tables(NH, HD ** -0.5) + rope_tables(NKV, 1.0)):
        arrays[name] = table
    args = [nc.dram_tensor(name, a.shape, mybir.dt.from_np(a.dtype), kind="ExternalInput").ap() for name, a in arrays.items()]
    out = nc.dram_tensor("out", (B, S, D), F32, kind="ExternalOutput").ap()
    build(nc, *args, out)
    result = run_bass_kernel_spmd(nc, [arrays], core_ids=[0])
    return result.results[0]["out"]
```

```python
from contextlib import ExitStack

import numpy as np

import concourse.bass as bass
from concourse import mybir

ALU = mybir.AluOpType
ACT = mybir.ActivationFunctionType
F32 = mybir.dt.float32
BF16 = mybir.dt.bfloat16
F16 = mybir.dt.float16
AX_X = mybir.AxisListType.X

P = 128
B, S, D = 8, 512, 128
NH, NKV, HD = 16, 4, 8
E, TOPK, FF = 16, 4, 128
NT = S // P
NG = NH // NKV
EPS = 1e-5
ALPHA, LIMIT = 1.702, 7.0
NEG = -1.0e30
BIG = 3.0e38

Q_PART = (0, 0, 0, 1, 1, 2)
K_PART = (0, 1, 2, 0, 1, 0)
NR = len(Q_PART)
STACK = NR * HD

W_TOP = 1024.0
TINY = 1.0e-30

NU = NG * NT * 2
NV = NG * NT
NM = NG * 11
RING = 8
LAG = 4
M_SLOT0 = 5

JOBS = (("v", "m"), ("oT0", "tail"), ("xT", "p"), ("oT1", "tail"), ("mB", "m_prev"), ("q", "p"), ("oT2", "tail"), ("qr", "p"),
        ("oT3", "tail"), ("k", "p"), ("onT", "tail"), ("kr", "p"), ("y", "tail"), ("x2", "tail"), ("mA", "m"), ("lg", "tail"),
        ("rT", "tail"), ("bias", "tail"))


def stages(n):
    return {"e": 1 <= n <= B, "e_prev": 2 <= n <= B + 1, "m": 0 <= n < B, "m_prev": 1 <= n <= B, "p": n < B - 1, "tail": n >= 2}


def jobs_of(n):
    return [name for name, stage in JOBS if stages(n)[stage]]


class Step:

    def __init__(self, t, par, like):
        self.t, self.par = t, par
        has = stages(like)
        self.e, self.e_prev, self.m, self.m_prev, self.p, self.tail = (has[k] for k in ("e", "e_prev", "m", "m_prev", "p", "tail"))
        self.jobs = jobs_of(like)
        before = sum(len(jobs_of(n)) for n in range(-1, min(like, 2)))
        self.before = before + len(JOBS) * (t - 2) if 2 <= like <= B - 2 else before + sum(len(jobs_of(n)) for n in range(2, like))

    def filled(self, job):
        return self.before + self.jobs.index(job) + 1

    def free(self, job):
        return self.before + self.jobs.index(job)


def m_slot(m):
    return M_SLOT0 + m * NU // NM


def v_slot(n):
    return 2 * n + LAG


def m_unit(m):
    g, k = divmod(m, 11)
    if k == 0:
        return 0, NG * g, 4
    if k < 3:
        return 1, NG * g + 2 * (k - 1), 2
    return (2, NG * g + k - 3, 1) if k < 7 else (3, NG * g + k - 7, 1)


def m_units_of(st, u):
    before = [(m, st.t - 1, 1 - st.par) for m in range(NM) if m_slot(m) == u + NU and st.m_prev]
    return before + [(m, st.t, st.par) for m in range(NM) if m_slot(m) == u and st.m]


def values_of(st, u):
    before = [(n, st.t - 2, st.par) for n in range(NV) if v_slot(n) == u + NU and st.e_prev]
    return before + [(n, st.t - 1, 1 - st.par) for n in range(NV) if v_slot(n) == u and st.e]


def build(nc, x, wq, wk, wv, wo, router_w, router_b, gate_up, gate_up_b, down, down_b, cos_q, sin_q, cos_k, sin_k, out):
    with ExitStack() as ctx:
        def sb(name, shape, dt=F32):
            return ctx.enter_context(nc.sbuf_tensor(name, shape, dt))

        def sem(name):
            return ctx.enter_context(nc.semaphore(name))

        X = sb("X", [P, B * NT, D])
        x2T = sb("x2T", [P, 2, B * S], F16)
        route = sb("route", [P, B * NT, E])
        ident = sb("ident", [P, P])
        ident_bf = sb("ident_bf", [P, P], BF16)
        mask = sb("mask", [P, 4, P], BF16)
        wq_raw, wk_raw = sb("wq_raw", [P, NH * HD]), sb("wk_raw", [P, NKV * HD])
        wq_p, wq_r = sb("wq_p", [P, HD, NH]), sb("wq_r", [P, HD, NH])
        wk_p, wk_r = sb("wk_p", [P, HD, NKV]), sb("wk_r", [P, HD, NKV])
        wv_s, wo_s = sb("wv_s", [P, NKV * HD]), sb("wo_s", [P, D])
        rw_s, rb_s = sb("rw_s", [P, E]), sb("rb_s", [P, E])
        cosq_s, sinq_s = sb("cosq_s", [P, S]), sb("sinq_s", [P, S])
        cosk_s, sink_s = sb("cosk_s", [P, P]), sb("sink_s", [P, P])
        gu_s = sb("gu_s", [P, E, 2 * FF])
        dn_s = sb("dn_s", [P, E, D])
        dnb_s = sb("dnb_s", [E, D])
        gub_s = sb("gub_s", [P, E, 2])
        gate_b, up_b = sb("gate_b", [P, E]), sb("up_b", [P, E])
        w_abs, w_max, w_inv, w_neg, w_scale = (sb(n, [P, 1]) for n in ("w_abs", "w_max", "w_inv", "w_neg", "w_scale"))
        ones = sb("ones", [1, P])
        mhalf, limit = sb("mhalf", [P, NT]), sb("limit", [P, 1])
        stats, mv, veps, rstd = sb("stats", [P, NT, 6]), sb("mv", [P, NT, 2]), sb("veps", [P, NT]), sb("rstd", [P, NT])
        xn, xT = sb("xn", [P, NT, D]), sb("xT", [P, S])
        rope_c, rope_s, rope, left = sb("rope_c", [P, S]), sb("rope_s", [P, S]), sb("rope", [P, S]), sb("left", [P, S])
        qparts = sb("qparts", [P, 3, S], BF16)
        kparts = sb("kparts", [P, 3, P], BF16)
        Qs = [sb(f"Qs{i}", [P, NH, S], BF16) for i in range(2)]
        Ks = [sb(f"Ks{i}", [P, NKV, S], BF16) for i in range(2)]
        Km = [sb(f"Km{i}", [P, NKV, S], BF16) for i in range(2)]
        Vs = [sb(f"Vs{i}", [P, NT, NKV, 32]) for i in range(2)]
        probs = sb("probs", [P, RING, 2, S])
        negmax = sb("negmax", [P, NT, NH])
        mcast = sb("mcast", [P, 2, NT, 2, NH // 2], BF16)
        mparts = [sb(f"mparts{i}", [NH, S], BF16) for i in range(2)]
        oT = [sb(f"oT{i}", [P, NG, S]) for i in range(2)]
        rden, on = sb("rden", [P, NT, NH]), sb("on", [P, NT, D])
        onT = sb("onT", [P, S])
        x1 = sb("x1", [P, NT, D])
        stats2, mv2, veps2, rstd2 = sb("stats2", [P, NT, 6]), sb("mv2", [P, NT, 2]), sb("veps2", [P, NT]), sb("rstd2", [P, NT])
        x2n, x2s, x2hl = sb("x2n", [P, NT, D]), sb("x2s", [P, S]), sb("x2hl", [P, 2, S], F16)
        lg, top, first4, cut = sb("lg", [P, NT, 24]), sb("top", [P, NT, 8]), sb("first4", [P, NT, 8]), sb("cut", [P, NT, 24])
        ldiff, lexp, chosen, lsum, lrec = (sb(n, [P, NT, k]) for n, k in (("ldiff", E), ("lexp", E), ("chosen", E), ("lsum", 1), ("lrec", 1)))
        wsel, rt = sb("wsel", [P, NT, E]), sb("rt", [P, NT, E])
        gu_hl = Qs[0][:].bitcast(F16).rearrange("p e (two w f) -> p e two w f", two=2, w=2)
        rtT = left[0:E, :]

        ps_e = ctx.enter_context(nc.psum_tensor("ps_e", [P, 2, 2, S], F32))
        ps_m = ctx.enter_context(nc.psum_tensor("ps_m", [P, 2, S], F32))
        ps_o = ctx.enter_context(nc.psum_tensor("ps_o", [P, S], F32))
        ps_x = ctx.enter_context(nc.psum_tensor("ps_x", [P, S], F32))

        q_dram = nc.dram_tensor("q_dram", [2, NR, P, S], BF16, kind="Internal").ap()
        k_dram = nc.dram_tensor("k_dram", [2, NR, NKV * HD, S], BF16, kind="Internal").ap()

        x_first, x_rest, wq_in, w_in, moe_in, const_rdy = sem("x_first"), sem("x_rest"), sem("wq_in"), sem("w_in"), sem("moe_in"), sem("const_rdy")
        init, perm, zero_v, biases = sem("init"), sem("perm"), sem("zero_v"), sem("biases")
        zero_g = sem("zero_g")
        st_done, mv_done, ve_done, rs_done, xn_done = (sem(n) for n in ("st_done", "mv_done", "ve_done", "rs_done", "xn_done"))
        x_fill, x_read = sem("x_fill"), sem("x_read")
        rope_add = sem("rope_add")
        part_a, part_r, part_b, part_c = sem("part_a"), sem("part_r"), sem("part_b"), sem("part_c")
        q_spill, k_spill = sem("q_spill"), sem("k_spill")
        stack_in = sem("stack_in")
        mx_mm, mx_red = sem("mx_mm"), sem("mx_red")
        mh_done, ml_done, m_in = sem("mh_done"), sem("ml_done"), sem("m_in")
        sc_mm, exp_done, causal = sem("sc_mm"), sem("exp_done"), sem("causal")
        pv_mm, o_ev = sem("pv_mm"), sem("o_ev")
        rden_done = sem("rden_done")
        st2_done, mv2_done, ve2_done, rs2_done, x2n_done = (sem(n) for n in ("st2_done", "mv2_done", "ve2_done", "rs2_done", "x2n_done"))
        x2_kept, top_done, first_done, diff_done, lexp_done = (sem(n) for n in ("x2_kept", "top_done", "first_done", "diff_done", "lexp_done"))
        cut_done, chosen_done, wsel_done, lsum_done, lrec_done, rt_done, rt_kept = (
            sem(n) for n in ("cut_done", "chosen_done", "wsel_done", "lsum_done", "lrec_done", "rt_done", "rt_kept"))

        def wait(eng, s, value):
            if not isinstance(value, int) or value > 0:
                eng.wait_ge(s, value)

        def tiles(t):
            return bass.ds(t * NT, NT)

        def steps(eng, step):
            for t in (-1, 0, 1):
                step(Step(t, t % 2, t))
            with eng.Fori(2, 5, 2) as t:
                step(Step(t, 0, 2))
                step(Step(t + 1, 1, 3))
            for t in range(B - 2, B + 2):
                step(Step(t, t % 2, t))

        gate_mm, up_mm, relu_done, low_done, v_done, glu_done = (sem(n) for n in ("gate_mm", "up_mm", "relu_done", "low_done", "v_done", "glu_done"))
        act_done, down_mm, acc_done, rc_done, out_done = (sem(n) for n in ("act_done", "down_mm", "acc_done", "rc_done", "out_done"))
        max_done, flip_done, top_w, spread_done, scale_done = (sem(n) for n in ("max_done", "flip_done", "top_w", "spread_done", "scale_done"))
        high_w, low_w, x2h_done, x2l_done = sem("high_w"), sem("low_w"), sem("x2h_done"), sem("x2l_done")
        rc, acc = sb("rc", [P, NT, E]), x1
        UNITS, NB = B * E, 4

        def turns(eng, turn, lag):
            for n in range(E):
                turn(0, n)
            with eng.Fori(1, B) as c:
                for e in range(E):
                    turn(c, e)
            for n in range(lag):
                turn(B, n)

        def unit(c, e, back):
            if isinstance(c, int) and not 0 <= E * c + e - back < UNITS:
                return None
            chunk, expert = (c, e - back) if e >= back else (c - 1, e - back + E)
            return chunk, expert, E * chunk + expert

        def ps_gate(e):
            return ps_e[:, e % 2, 0, :]

        def ps_up(e):
            return ps_e[:, e % 2, 1, :]

        def ps_down(e):
            return (ps_m[:, 0, :], ps_m[:, 1, :], ps_o[:], ps_x[:])[e % NB]

        def glu_s(e):
            return probs[:, e % NB, 0, :]

        def low_s(e):
            return probs[:, e % NB, 1, :]

        def act_s(e):
            return probs[:, NB + e % NB, 0, :]

        def pe_experts(pe):
            mm = nc.tensor.matmul
            pe.wait_ge(x2_kept, B)
            pe.wait_ge(low_w, NT)
            pe.wait_ge(o_ev, NG * B)
            pe.wait_ge(x_read, Step(B + 1, 1, B + 1).filled("bias"))

            def three(psum, e, which, c):
                for k, (wp, xp) in enumerate(((0, 0), (0, 1), (1, 0))):
                    last = mm(psum, gu_hl[:, e, wp, which, :], x2T[:, xp, bass.ds(c * S, S)], start=(k == 0), stop=(k == 2))
                return last

            def turn(c, e):
                if unit(c, e, 0):
                    n = E * c + e
                    wait(pe, relu_done, n - 1)
                    three(ps_gate(e), e, 0, c).then_inc(gate_mm, 1)
                    wait(pe, low_done, n - 1)
                    three(ps_up(e), e, 1, c).then_inc(up_mm, 1)
                back = unit(c, e, 3)
                if back:
                    _, x, m = back
                    pe.wait_ge(act_done, m + 1)
                    wait(pe, acc_done, m - NB + 1)
                    for i in range(NT):
                        last = mm(ps_down(x)[:, D * i:D * (i + 1)], act_s(x)[:, P * i:P * (i + 1)], dn_s[:, x, :], start=True, stop=True)
                    last.then_inc(down_mm, 1)

            turns(pe, turn, 3)

        def act_experts(act):
            a = nc.scalar
            act.wait_ge(const_rdy, 5)

            def turn(c, e):
                back = unit(c, e, 1)
                if back:
                    _, x, m = back
                    act.wait_ge(relu_done, m + 1)
                    a.activation(glu_s(x), glu_s(x), ACT.Gelu_apprx_sigmoid, bias=limit[:], scale=-1.0).then_inc(glu_done, 1)
                if unit(c, e, 0):
                    n = E * c + e
                    act.wait_ge(gate_mm, n + 1)
                    wait(act, act_done, n - NB + 1)
                    a.activation(glu_s(e), ps_gate(e), ACT.Relu, bias=gate_b[:, e:e + 1], scale=w_neg[:]).then_inc(relu_done, 1)
                    act.wait_ge(up_mm, n + 1)
                    a.activation(low_s(e), ps_up(e), ACT.Relu, bias=up_b[:, e:e + 1], scale=w_neg[:]).then_inc(low_done, 1)

            turns(act, turn, 1)

        def pool_experts(pool):
            def turn(c, e):
                if unit(c, e, 0):
                    n = E * c + e
                    pool.wait_ge(low_done, n + 1)
                    pool.nop(nofuse=True)
                    nc.gpsimd.tensor_scalar(low_s(e), low_s(e), 2 * LIMIT, None, ALU.min).then_inc(v_done, 1)

            turns(pool, turn, 0)

        def dve_experts(dve):
            v = nc.vector
            dve.wait_ge(rt_kept, B)

            def turn(c, e):
                back = unit(c, e, 2)
                if back:
                    _, x, m = back
                    dve.wait_ge(glu_done, m + 1)
                    dve.wait_ge(v_done, m + 1)
                    wait(dve, down_mm, m - NB + 1)
                    v.scalar_tensor_tensor(out=act_s(x), in0=low_s(x), scalar=LIMIT + 1.0, in1=glu_s(x),
                                           op0=ALU.subtract, op1=ALU.mult).then_inc(act_done, 1)
                back = unit(c, e, 4)
                if back:
                    chunk, x, m = back
                    if x == 0:
                        wait(dve, acc_done, m)
                        v.tensor_scalar(rc[:], route[:, tiles(chunk), :], -1.0, None, ALU.mult).then_inc(rc_done, 1)
                        dve.wait_ge(rc_done, chunk + 1)
                    dve.wait_ge(down_mm, m + 1)
                    wait(dve, acc_done, m)
                    for i in range(NT):
                        here = X[:, bass.ds(chunk * NT + i, 1), :].rearrange("p a d -> p (a d)")
                        last = v.scalar_tensor_tensor(out=here if x == E - 1 else acc[:, i, :], in0=ps_down(x)[:, D * i:D * (i + 1)],
                                                      scalar=rc[:, i, x:x + 1], in1=here if x == 0 else acc[:, i, :],
                                                      op0=ALU.mult, op1=ALU.add)
                    last.then_inc(acc_done, 1)

            turns(dve, turn, 4)

        block = ctx.enter_context(nc.Block())

        @block.sync
        def _(sp):
            sp.dma_start(X[:, 0:NT, :], x[0].rearrange("(i p) d -> p i d", p=P)).then_inc(x_first, 16)
            sp.dma_start(wq_raw[:], wq).then_inc(wq_in, 16)
            sp.dma_start(wk_raw[:], wk).then_inc(wq_in, 16)
            sp.dma_start(wv_s[:], wv).then_inc(w_in, 16)
            sp.dma_start(cosq_s[:], cos_q).then_inc(w_in, 16)
            sp.dma_start(sinq_s[:], sin_q).then_inc(w_in, 16)
            sp.dma_start(cosk_s[:], cos_k).then_inc(w_in, 16)
            sp.dma_start(sink_s[:], sin_k).then_inc(w_in, 16)
            sp.dma_start(wo_s[:], wo).then_inc(w_in, 16)
            sp.dma_start(X[:, NT:B * NT, :], x[1:B].rearrange("b (i p) d -> p (b i) d", p=P)).then_inc(x_rest, 16)
            sp.dma_start(rw_s[:], router_w).then_inc(moe_in, 16)
            sp.dma_start(rb_s[:], router_b.unsqueeze(0).to_broadcast([P, E])).then_inc(moe_in, 16)
            sp.dma_start(dnb_s[:], down_b).then_inc(moe_in, 16)
            sp.dma_start(gub_s[:], gate_up_b.rearrange("e (f two) -> f e two", two=2)).then_inc(moe_in, 16)
            sp.dma_start(gu_s[:], gate_up.rearrange("e h f -> h e f")).then_inc(moe_in, 16)
            sp.dma_start(dn_s[:], down.rearrange("e f h -> f e h")).then_inc(moe_in, 16)
            sp.wait_ge(zero_v, 9)
            sp.wait_ge(zero_g, 8)

            def load_max(st, batch, par, half):
                sp.wait_ge(x_read, st.filled("mB" if half else "mA"))
                heads = slice(8 * half, 8 * half + 8)
                sp.dma_start(Qs[par][STACK:STACK + 1, heads, :], mparts[half][0:8]).then_inc(m_in, 16)
                sp.dma_start(Qs[par][STACK + 1:STACK + 2, heads, :], mparts[half][8:16]).then_inc(m_in, 16)

            def step(st):
                t, par, nxt = st.t, st.par, 1 - st.par
                if st.m_prev:
                    load_max(st, t - 1, 1 - par, 1)
                if st.p:
                    sp.wait_ge(part_c, 2 * (t + 1) + 1)
                    for r in range(NR):
                        sp.dma_start(q_dram[nxt, r], qparts[:, Q_PART[r], :]).then_inc(q_spill, 16)
                    sp.wait_ge(part_c, 2 * (t + 1) + 2)
                    for r in range(NR):
                        sp.dma_start(k_dram[nxt, r].rearrange("q (i c) -> i q c", i=NT), kparts[:, K_PART[r], :]).then_inc(k_spill, 16)
                if st.m:
                    load_max(st, t, par, 0)
                if st.p:
                    wait(sp, mx_mm, NM * t)
                    sp.wait_ge(k_spill, 96 * (t + 2))
                    k_flat = k_dram[nxt].rearrange("r (d h) t -> (r d) h t", d=HD)
                    sp.dma_start(Km[nxt][0:STACK], k_flat).then_inc(stack_in, 16)
                    wait(sp, sc_mm, NU * t)
                    sp.wait_ge(q_spill, 96 * (t + 2))
                    q_flat = q_dram[nxt].rearrange("r (d h) t -> (r d) h t", d=HD)
                    sp.dma_start(Qs[nxt][0:STACK], q_flat).then_inc(stack_in, 16)
                    sp.dma_start(Ks[nxt][0:STACK], k_flat).then_inc(stack_in, 16)

            steps(sp, step)
            with sp.Fori(0, B) as c:
                sp.wait_ge(acc_done, E * c + E)
                sp.dma_start(out[bass.ds(c, 1)].rearrange("a (i p) d -> p (a i) d", p=P), X[:, tiles(c), :]).then_inc(out_done, 16)
            sp.wait_ge(out_done, 16 * B)

        @block.gpsimd
        def _(pool):
            g = nc.gpsimd
            g.memset(mhalf[:], -0.5).then_inc(const_rdy, 1)
            g.memset(limit[:], LIMIT).then_inc(const_rdy, 1)
            g.memset(ones[:], 1.0).then_inc(const_rdy, 1)
            g.memset(ident[:], 0.0).then_inc(init, 1)
            g.memset(mask[:], 0.0).then_inc(init, 1)
            pool.wait_ge(init, 2)
            g.affine_select(out=ident[:], in_=ident[:], compare_op=ALU.not_equal, fill=1.0, base=0,
                            pattern=[[-1, P]], channel_multiplier=1).then_inc(init, 1)
            g.affine_select(out=mask[:], in_=mask[:], compare_op=ALU.is_ge, fill=NEG, base=0,
                            pattern=[[0, 4], [-1, P]], channel_multiplier=1).then_inc(const_rdy, 1)
            pool.wait_ge(init, 3)
            g.tensor_copy(ident_bf[:], ident[:]).then_inc(const_rdy, 1)

            def clear():
                g.memset(Qs[1][:].bitcast(F32), 0.0).then_inc(zero_g, 1)
                g.memset(Km[1][:].bitcast(F32), 0.0).then_inc(zero_g, 1)
                g.memset(Ks[1][:].bitcast(F32), 0.0).then_inc(zero_g, 1)
                g.memset(Vs[1][:], 0.0).then_inc(zero_g, 1)
                g.memset(lg[:], BIG).then_inc(zero_g, 1)
                g.memset(first4[:], BIG).then_inc(zero_g, 1)
                pool.wait_ge(zero_g, 6)
                g.memset(Vs[1][:, :, :, HD:HD + 1], 1.0).then_inc(zero_g, 1)
                pool.wait_ge(zero_g, 7)
                g.memset(Ks[1][32:64], 1.0).then_inc(zero_g, 1)
                pool.wait_ge(zero_g, 8)

            def step(st):
                t = st.t
                for u in range(NU):
                    if st.e:
                        pool.wait_ge(exp_done, NU * (t - 1) + u + 1)
                        pool.nop(nofuse=True)
                        diag = probs[:, u % RING, :, 0:P]
                        g.affine_select(out=diag, in_=diag, compare_op=ALU.is_ge, fill=0.0, base=0,
                                        pattern=[[0, 2], [1, P]], channel_multiplier=-1).then_inc(causal, 1)
                    if st.p and u == 1:
                        pool.wait_ge(ve_done, t + 2)
                        g.tensor_tensor(rstd[:], veps[:], mhalf[:], ALU.pow).then_inc(rs_done, 1)
                    if isinstance(t, int) and t == -1 and u == 2:
                        clear()
                    for part, (add, less, rest) in ((0, (10, 12, 14)), (1, (15, 17, 19))):
                        cols, parts = (slice(0, P if part else S), kparts if part else qparts)
                        if st.p and u == add:
                            pool.wait_ge(x_read, st.filled("kr" if part else "qr"))
                            if part:
                                pool.wait_ge(part_c, 2 * (t + 1) + 1)
                            g.tensor_tensor(rope[:, cols], rope_c[:, cols], rope_s[:, cols], ALU.add).then_inc(rope_add, 1)
                        if st.p and u == less:
                            pool.wait_ge(part_a, 2 * (t + 1) + part + 1)
                            g.tensor_tensor(left[:, cols], rope[:, cols], parts[:, 0, :], ALU.subtract).then_inc(part_r, 1)
                        if st.p and u == rest:
                            pool.wait_ge(part_b, 2 * (t + 1) + part + 1)
                            g.tensor_tensor(parts[:, 2, :], left[:, cols], parts[:, 1, :], ALU.subtract).then_inc(part_c, 1)
                    if st.tail and u == 16:
                        pool.wait_ge(ve2_done, t - 1)
                        g.tensor_tensor(rstd2[:], veps2[:], mhalf[:], ALU.pow).then_inc(rs2_done, 1)
                    if st.tail and u == 21:
                        pool.wait_ge(x2h_done, t - 1)
                        g.tensor_tensor(x2hl[:, 1, :], x2s[:], x2hl[:, 0, :], ALU.subtract).then_inc(x2l_done, 1)
                    if st.tail and u == 28:
                        pool.wait_ge(rt_done, t - 1)
                        g.tensor_copy(route[:, tiles(t - 2), :], rt[:]).then_inc(rt_kept, 1)

            steps(pool, step)
            pool_experts(pool)

        @block.tensor
        def _(pe):
            mm = nc.tensor.matmul
            pe.wait_ge(const_rdy, 5)
            pe.wait_ge(perm, 6)

            def turn(job, st, source, rows=P):
                pe.wait_ge(x_read, st.free(job))
                for i in range(NT):
                    last = nc.tensor.transpose(ps_x[0:rows, P * i:P * (i + 1)], source(i), ident[:])
                last.then_inc(x_fill, 1)

            def product(job, st, left_side, right_side, width):
                pe.wait_ge(x_read, st.free(job))
                for i in range(NT):
                    last = mm(ps_x[:, width * i:width * (i + 1)], left_side[:, P * i:P * (i + 1)], right_side[:], start=True, stop=True)
                last.then_inc(x_fill, 1)

            def project(job, st, rows, w):
                pe.wait_ge(x_read, st.free(job))
                for i in range(P // rows):
                    n = S * rows // P
                    last = mm(ps_x[rows * i:rows * (i + 1), 0:n], w[:], xT[:, n * i:n * (i + 1)], start=True, stop=True)
                last.then_inc(x_fill, 1)

            def turn_max(job, st, half):
                pe.wait_ge(x_read, st.free(job))
                for i in range(NT):
                    last = mm(ps_x[0:NH, P * i:P * (i + 1)], mcast[:, half, i].rearrange("p c h -> p (c h)"), ident_bf[:], start=True, stop=True)
                last.then_inc(x_fill, 1)

            def step(st):
                t, par = st.t, st.par
                if isinstance(t, int) and t == 1:
                    pe.wait_ge(moe_in, 16 * 6)
                if isinstance(t, int) and t == B + 1:
                    pe.wait_ge(max_done, 1)
                    pe.wait_ge(mx_red, NM * B)
                    nc.tensor.transpose(ps_m[0:1, 0, 0:P], w_abs[:], ident[:]).then_inc(flip_done, 1)
                    pe.wait_ge(top_w, 1)
                    mm(ps_m[:, 1, 0:1], ones[:], w_max[0:1, :], start=True, stop=True).then_inc(spread_done, 1)
                for u in range(NU):
                    if st.e:
                        g, j, pair = u // 8, u // 2 % NT, u % 2
                        if u in (0, NU // 2):
                            pe.wait_ge(m_in, 64 * (t - 1) + (32 if u == 0 else 64))
                        wait(pe, exp_done, NU * (t - 1) + u - 1)
                        for k in range(2):
                            h = NG * g + 2 * pair + k
                            last = mm(ps_e[:, u % 2, k, 0:S - P * j], Ks[1 - par][:, h % NKV, P * j:P * (j + 1)],
                                      Qs[1 - par][:, h, P * j:S], start=True, stop=True)
                        last.then_inc(sc_mm, 1)
                    for n, batch, bpar in values_of(st, u):
                        g, j = n // NT, n % NT
                        if j == 0:
                            wait(pe, o_ev, NG * batch + g)
                        pe.wait_ge(causal, NU * batch + 2 * n + 2)
                        for k in range(4):
                            last = mm(ps_o[32 * k:32 * k + 32, P * j:S], Vs[bpar][:, j, k, :],
                                      probs[:, (2 * n + k // 2) % RING, k % 2, 0:S - P * j],
                                      start=(j == 0), stop=(j == NT - 1))
                        last.then_inc(pv_mm, 1)
                    if st.m and u == 2:
                        pe.wait_ge(x_read, st.free("v"))
                        for i in range(NT):
                            last = mm(ps_x[:, 32 * i:32 * i + 32], xT[:, P * i:P * (i + 1)], wv_s[:], start=True, stop=True)
                        last.then_inc(x_fill, 1)
                    if st.tail and u in (3, 5, 8, 10):
                        i = (3, 5, 8, 10).index(u)
                        pe.wait_ge(o_ev, NG * (t - 1))
                        turn(f"oT{i}", st, lambda g: oT[par][:, g, P * i:P * (i + 1)])
                    if st.p and u == 4:
                        pe.wait_ge(xn_done, t + 2)
                        turn("xT", st, lambda i: xn[:, i, :])
                    if st.m_prev and u == 6:
                        pe.wait_ge(ml_done, 2 * t)
                        turn_max("mB", st, 1)
                    if st.p and u == 7:
                        pe.wait_ge(x_read, st.filled("xT"))
                        project("q", st, P, wq_p)
                    if st.p and u == 9:
                        project("qr", st, P, wq_r)
                    if st.p and u == 11:
                        project("k", st, 32, wk_p)
                    if st.tail and u == 12:
                        pe.wait_ge(x_read, st.filled("oT3"))
                        turn("onT", st, lambda i: on[:, i, :])
                    if st.p and u == 13:
                        project("kr", st, 32, wk_r)
                    if st.tail and u == 14:
                        pe.wait_ge(x_read, st.filled("onT"))
                        product("y", st, onT, wo_s, D)
                    if st.tail and u == 20:
                        pe.wait_ge(x2n_done, t - 1)
                        turn("x2", st, lambda i: x2n[:, i, :])
                    if st.m and u == 22:
                        pe.wait_ge(ml_done, 2 * t + 1)
                        turn_max("mA", st, 0)
                    if st.tail and u == 23:
                        pe.wait_ge(x_read, st.filled("x2"))
                        product("lg", st, x2s, rw_s, E)
                    if st.tail and u == 28:
                        pe.wait_ge(rt_done, t - 1)
                        turn("rT", st, lambda i: rt[:, i, :], rows=E)
                    if st.tail and u == 30:
                        pe.wait_ge(x_read, st.filled("rT"))
                        product("bias", st, rtT, dnb_s, D)
                    for m, batch, bpar in m_units_of(st, u):
                        i, h0, nh = m_unit(m)
                        w = P * (i + 1)
                        if m == 0:
                            pe.wait_ge(stack_in, 48 * (batch + 1))
                        wait(pe, mx_red, NM * batch + m - 1)
                        bank = ps_m[:, m % 2, 0:nh * w].rearrange("p (h k) -> p h k", h=nh)
                        mm(bank[:, :, P * i:w], ident_bf[:], mask[:, 0:nh, :], start=True, stop=False, skip_group_check=True)
                        for k in range(nh):
                            h = h0 + k
                            last = mm(bank[:, k, :], Qs[bpar][:, h, P * i:w], Km[bpar][:, h % NKV, 0:w],
                                      start=False, stop=True, skip_group_check=True)
                        last.then_inc(mx_mm, 1)

            steps(pe, step)
            pe_experts(pe)

        @block.scalar
        def _(act):
            a = nc.scalar

            def step(st):
                t, par = st.t, st.par
                for u in range(NU):
                    if st.e:
                        j = u // 2 % NT
                        wait(act, pv_mm, NV * (t - 1) + (u - RING) // 2 + 1)
                        act.wait_ge(sc_mm, NU * (t - 1) + u + 1)
                        a.activation(probs[:, u % RING, :, 0:S - P * j], ps_e[:, u % 2, :, 0:S - P * j],
                                     ACT.Exp).then_inc(exp_done, 1)
                    for n, batch, bpar in values_of(st, u):
                        if n % NT == NT - 1:
                            g = n // NT
                            act.wait_ge(pv_mm, NV * batch + n + 1)
                            a.activation(oT[bpar][:, g, :], ps_o[:], ACT.Copy).then_inc(o_ev, 1)
                    if st.m and u == 2:
                        if isinstance(t, int) and t == 0:
                            act.wait_ge(zero_v, 9)
                            act.wait_ge(zero_g, 8)
                        wait(act, pv_mm, NV * (t - 1))
                        act.wait_ge(x_fill, st.filled("v"))
                        a.activation(Vs[par][:, :, :, 0:HD], ps_x[:, 0:NT * 32].rearrange("p (i k d) -> p i k d", i=NT, d=HD),
                                     ACT.Copy).then_inc(x_read, 1)
                    if st.p and u == 4:
                        act.wait_ge(x_fill, st.filled("xT"))
                        a.activation(xT[:], ps_x[:], ACT.Copy).then_inc(x_read, 1)
                    for job, slot, batch, half in (("mB", 6, t - 1, 1), ("mA", 22, t, 0)):
                        if u == slot and job in st.jobs:
                            act.wait_ge(x_fill, st.filled(job))
                            wait(act, m_in, 64 * batch + 32 * half)
                            a.activation(mparts[half][:], ps_x[0:NH], ACT.Copy).then_inc(x_read, 1)
                    if st.p and u in (11, 16):
                        w, parts, n = (S, qparts, 1) if u == 11 else (P, kparts, 2)
                        wait(act, q_spill if u == 11 else k_spill, 96 * (t + 1))
                        act.wait_ge(rope_add, 2 * (t + 1) + n)
                        a.activation(parts[:, 0, :], rope[:, 0:w], ACT.Copy).then_inc(part_a, 1)
                    if st.p and u in (13, 18):
                        w, parts, n = (S, qparts, 1) if u == 13 else (P, kparts, 2)
                        act.wait_ge(part_r, 2 * (t + 1) + n)
                        a.activation(parts[:, 1, :], left[:, 0:w], ACT.Copy).then_inc(part_b, 1)
                    if st.tail and u == 12:
                        act.wait_ge(x_fill, st.filled("onT"))
                        a.activation(onT[:], ps_x[:], ACT.Copy).then_inc(x_read, 1)
                    if st.tail and u == 20:
                        act.wait_ge(x_fill, st.filled("x2"))
                        wait(act, x2_kept, t - 2)
                        a.activation(x2s[:], ps_x[:], ACT.Copy)
                        a.activation(x2hl[:, 0, :], ps_x[:], ACT.Copy).then_inc(x_read, 1)
                        act.wait_ge(x_read, st.filled("x2"))
                        act.sem_inc(x2h_done, 1)
                    if isinstance(t, int) and t == B + 1 and u in (13, 15, 17, 19):
                        q = slice(4 * ((u - 13) // 2), 4 * ((u - 13) // 2) + 4)
                        act.wait_ge(scale_done, 3)
                        act.wait_ge(sc_mm, NU * B)
                        a.activation(gu_hl[:, q, 0], gu_s[:, q, :].rearrange("p e (f w) -> p e w f", w=2), ACT.Copy,
                                     scale=w_scale[:]).then_inc(high_w, 1)
                    if st.tail and u == 25:
                        act.wait_ge(diff_done, t - 1)
                        a.activation(lexp[:], ldiff[:], ACT.Exp).then_inc(lexp_done, 1)
                    if st.tail and u == 28:
                        act.wait_ge(x_fill, st.filled("rT"))
                        a.activation(rtT[:], ps_x[0:E, :], ACT.Copy).then_inc(x_read, 1)

            steps(act, step)
            act_experts(act)

        @block.vector
        def _(dve):
            v = nc.vector
            dve.wait_ge(wq_in, 32)
            half = HD // 2
            for raw, plain, swapped, n in ((wq_raw, wq_p, wq_r, NH), (wk_raw, wk_p, wk_r, NKV)):
                cols = raw[:].rearrange("p (h d) -> p d h", d=HD)
                v.tensor_copy(plain[:], cols).then_inc(perm, 1)
                v.tensor_copy(swapped[:, 0:half, :], cols[:, half:HD, :]).then_inc(perm, 1)
                v.tensor_copy(swapped[:, half:HD, :], cols[:, 0:half, :]).then_inc(perm, 1)
            dve.wait_ge(x_first, 16)

            def clear(u):
                if u == 6:
                    dve.wait_ge(w_in, 16 * 6)
                if u in (4, 5, 8, 9):
                    k = (4, 5, 8, 9).index(u)
                    v.memset(Qs[0][:, 4 * k:4 * k + 4].bitcast(F32), 0.0).then_inc(zero_v, 1)
                if u == 10:
                    v.memset(Km[0][:].bitcast(F32), 0.0).then_inc(zero_v, 1)
                if u == 12:
                    v.memset(Ks[0][:].bitcast(F32), 0.0).then_inc(zero_v, 1)
                if u == 14:
                    v.memset(Vs[0][:], 0.0).then_inc(zero_v, 1)
                    dve.wait_ge(zero_v, 7)
                    v.memset(Vs[0][:, :, :, HD:HD + 1], 1.0).then_inc(zero_v, 1)
                    v.memset(Ks[0][32:64], 1.0).then_inc(zero_v, 1)

            def step(st):
                t, par = st.t, st.par
                if isinstance(t, int) and t == 1:
                    dve.wait_ge(moe_in, 16 * 6)
                    v.tensor_scalar(gate_b[:], gub_s[:, :, 0], -1.0, LIMIT, ALU.mult, ALU.add).then_inc(biases, 1)
                    v.tensor_scalar(up_b[:], gub_s[:, :, 1], -1.0, LIMIT, ALU.mult, ALU.add).then_inc(biases, 1)
                    dve.wait_ge(zero_g, 8)
                if isinstance(t, int) and t == B + 1:
                    dve.wait_ge(flip_done, 1)
                    v.tensor_reduce(w_max[0:1, :], ps_m[0:1, 0, 0:P], AX_X, ALU.max).then_inc(top_w, 1)
                    dve.wait_ge(spread_done, 1)
                    v.tensor_scalar(w_inv[:], ps_m[:, 1, 0:1], TINY, 1.0 / W_TOP, ALU.max, ALU.mult).then_inc(scale_done, 1)
                    dve.wait_ge(scale_done, 1)
                    v.tensor_scalar(w_neg[:], w_inv[:], -1.0, None, ALU.mult).then_inc(scale_done, 1)
                    v.reciprocal(w_scale[:], w_inv[:]).then_inc(scale_done, 1)
                for u in range(NU):
                    if isinstance(t, int) and t == -1:
                        clear(u)
                    if isinstance(t, int) and t == B and u == 12:
                        v.tensor_reduce(w_abs[:], gu_s[:].rearrange("p e f -> p (e f)"), AX_X, ALU.max, apply_absolute_value=True).then_inc(max_done, 1)
                    if isinstance(t, int) and t == B + 1 and u in (14, 16, 18, 20):
                        k = (u - 14) // 2
                        q = slice(4 * k, 4 * k + 4)
                        dve.wait_ge(scale_done, 3)
                        dve.wait_ge(high_w, k + 1)
                        last = None
                        for w in range(2):
                            last = v.scalar_tensor_tensor(out=gu_hl[:, q, 1, w, :], in0=gu_s[:, q, w:2 * FF:2], scalar=w_scale[:],
                                                          in1=gu_hl[:, q, 0, w, :], op0=ALU.mult, op1=ALU.subtract)
                        last.then_inc(low_w, 1)
                    if st.tail and u == 26:
                        dve.wait_ge(x2l_done, t - 1)
                        v.tensor_copy(x2T[:, :, bass.ds((t - 2) * S, S)], x2hl[:]).then_inc(x2_kept, 1)
                    if st.p and u == 0:
                        if isinstance(t, int) and t == 0:
                            dve.wait_ge(x_rest, 16)
                        for i in range(NT):
                            last = v.bn_stats(stats[:, i, :], X[:, bass.ds((t + 1) * NT + i, 1), :].rearrange("p a d -> p (a d)"))
                        last.then_inc(st_done, 1)
                        dve.wait_ge(st_done, t + 2)
                        dve.nop(nofuse=True)
                        for i in range(NT):
                            last = v.bn_aggr(mv[:, i, :], stats[:, i, :])
                        last.then_inc(mv_done, 1)
                        dve.wait_ge(mv_done, t + 2)
                        v.tensor_scalar(veps[:], mv[:, :, 1], EPS, None, ALU.add).then_inc(ve_done, 1)
                    if st.p and u == 3:
                        dve.wait_ge(rs_done, t + 2)
                        for i in range(NT):
                            src = X[:, bass.ds((t + 1) * NT + i, 1), :].rearrange("p a d -> p (a d)")
                            last = v.tensor_scalar(xn[:, i, :], src, mv[:, i, 0:1], rstd[:, i:i + 1], ALU.subtract, ALU.mult)
                        last.then_inc(xn_done, 1)
                    if st.tail and u in (3, 5, 8, 10):
                        i = (3, 5, 8, 10).index(u)
                        dve.wait_ge(x_fill, st.filled(f"oT{i}"))
                        heads = ps_x[:].rearrange("p (h w) -> p h w", w=32)
                        v.reciprocal(rden[:, i, :], heads[:, :, HD]).then_inc(rden_done, 1)
                        dve.wait_ge(rden_done, NT * (t - 2) + i + 1)
                        v.tensor_tensor(on[:, i, :].rearrange("p (h d) -> p h d", d=HD), heads[:, :, 0:HD],
                                        rden[:, i, :].unsqueeze(2).to_broadcast([P, NH, HD]), ALU.mult).then_inc(x_read, 1)
                    for exists, slot, batch, half in ((st.m_prev, 5, t - 1, 1), (st.m, 21, t, 0)):
                        if u == slot and exists:
                            dve.wait_ge(mx_red, NM * batch + NM // 2 * (half + 1))
                            exact = negmax[:, :, 8 * half:8 * half + 8]
                            v.tensor_copy(mcast[:, half, :, 0, :], exact).then_inc(mh_done, 1)
                            dve.wait_ge(mh_done, 2 * batch + half + 1)
                            v.tensor_tensor(mcast[:, half, :, 1, :], exact, mcast[:, half, :, 0, :], ALU.subtract).then_inc(ml_done, 1)
                    if st.p and u in (7, 9, 11, 13):
                        job, w, table, to = {7: ("q", S, cosq_s, rope_c), 9: ("qr", S, sinq_s, rope_s),
                                             11: ("k", P, cosk_s, rope_c), 13: ("kr", P, sink_s, rope_s)}[u]
                        if u == 11:
                            dve.wait_ge(rope_add, 2 * (t + 1) + 1)
                        dve.wait_ge(x_fill, st.filled(job))
                        v.tensor_tensor(to[:, 0:w], ps_x[:, 0:w], table[:], ALU.mult).then_inc(x_read, 1)
                    if st.tail and u == 14:
                        dve.wait_ge(x_fill, st.filled("y"))
                        v.tensor_tensor(x1[:], X[:, tiles(t - 2), :], ps_x[:].rearrange("p (i d) -> p i d", d=D), ALU.add).then_inc(x_read, 1)
                    if st.tail and u == 15:
                        dve.wait_ge(x_read, st.filled("y"))
                        for i in range(NT):
                            last = v.bn_stats(stats2[:, i, :], x1[:, i, :])
                        last.then_inc(st2_done, 1)
                        dve.wait_ge(st2_done, t - 1)
                        dve.nop(nofuse=True)
                        for i in range(NT):
                            last = v.bn_aggr(mv2[:, i, :], stats2[:, i, :])
                        last.then_inc(mv2_done, 1)
                        dve.wait_ge(mv2_done, t - 1)
                        v.tensor_scalar(veps2[:], mv2[:, :, 1], EPS, None, ALU.add).then_inc(ve2_done, 1)
                    if st.tail and u == 18:
                        dve.wait_ge(rs2_done, t - 1)
                        for i in range(NT):
                            last = v.tensor_scalar(x2n[:, i, :], x1[:, i, :], mv2[:, i, 0:1], rstd2[:, i:i + 1], ALU.subtract, ALU.mult)
                        last.then_inc(x2n_done, 1)
                    if st.tail and u == 23:
                        dve.wait_ge(x_fill, st.filled("lg"))
                        v.tensor_tensor(lg[:, :, 0:E], ps_x[:, 0:NT * E].rearrange("p (i e) -> p i e", e=E),
                                        rb_s[:].unsqueeze(1).to_broadcast([P, NT, E]), ALU.add).then_inc(x_read, 1)
                    if st.tail and u == 24:
                        dve.wait_ge(x_read, st.filled("lg"))
                        dve.nop(nofuse=True)
                        for i in range(NT):
                            last = v.max(top[:, i, :], lg[:, i, 0:E])
                        last.then_inc(top_done, 1)
                        dve.wait_ge(top_done, t - 1)
                        v.tensor_tensor(ldiff[:], lg[:, :, 0:E], top[:, :, 0:1].to_broadcast([P, NT, E]), ALU.subtract).then_inc(diff_done, 1)
                        v.tensor_copy(first4[:, :, 0:TOPK], top[:, :, 0:TOPK]).then_inc(first_done, 1)
                    if st.tail and u == 25:
                        dve.wait_ge(first_done, t - 1)
                        dve.nop(nofuse=True)
                        for i in range(NT):
                            last = v.match_replace(cut[:, i, :], first4[:, i, :], lg[:, i, :], -BIG)
                        last.then_inc(cut_done, 1)
                        dve.wait_ge(cut_done, t - 1)
                        v.tensor_tensor(chosen[:], cut[:, :, 0:E], lg[:, :, 0:E], ALU.not_equal).then_inc(chosen_done, 1)
                    if st.tail and u == 26:
                        dve.wait_ge(chosen_done, t - 1)
                        dve.wait_ge(lexp_done, t - 1)
                        v.tensor_tensor(wsel[:], lexp[:], chosen[:], ALU.mult).then_inc(wsel_done, 1)
                        dve.wait_ge(wsel_done, t - 1)
                        v.tensor_reduce(lsum[:], wsel[:], AX_X, ALU.add).then_inc(lsum_done, 1)
                    if st.tail and u == 27:
                        dve.wait_ge(lsum_done, t - 1)
                        v.reciprocal(lrec[:], lsum[:]).then_inc(lrec_done, 1)
                        dve.wait_ge(lrec_done, t - 1)
                        wait(dve, rt_kept, t - 2)
                        v.tensor_tensor(rt[:], wsel[:], lrec[:].to_broadcast([P, NT, E]), ALU.mult).then_inc(rt_done, 1)
                    if st.tail and u == 30:
                        dve.wait_ge(x_fill, st.filled("bias"))
                        v.tensor_tensor(X[:, tiles(t - 2), :], x1[:], ps_x[:].rearrange("p (i d) -> p i d", d=D), ALU.add).then_inc(x_read, 1)
                    for m, batch, bpar in m_units_of(st, u):
                        i, h0, nh = m_unit(m)
                        w = P * (i + 1)
                        dve.wait_ge(mx_mm, NM * batch + m + 1)
                        v.tensor_reduce(negmax[:, i, h0:h0 + nh], ps_m[:, m % 2, 0:nh * w].rearrange("p (h k) -> p h k", h=nh),
                                        AX_X, ALU.max, negate=True).then_inc(mx_red, 1)

            steps(dve, step)
            dve_experts(dve)


def rope_tables(heads, scale):
    half = HD // 2
    freq = (np.float32(1.0) / np.float32(10000.0) ** (np.arange(half, dtype=np.float32) / np.float32(half))).astype(np.float32)
    ang = np.arange(S, dtype=np.float32)[:, None] * freq[None, :]
    cos = np.concatenate([np.cos(ang), np.cos(ang)], 1).T * np.float32(scale)
    sin = np.concatenate([-np.sin(ang), np.sin(ang)], 1).T * np.float32(scale)
    rows = [np.repeat(t, heads, 0) for t in (cos, sin)]
    pieces = P // (heads * HD)
    return tuple(np.ascontiguousarray(np.concatenate(np.split(t, pieces, 1), 0), dtype=np.float32) for t in rows)


_INS = ["L0_attn_x", "L0_attn_wq", "L0_attn_wk", "L0_attn_wv", "L0_attn_wo", "L0_ffn_router_w", "L0_ffn_router_b",
        "L0_ffn_gate_up_proj", "L0_ffn_gate_up_bias", "L0_ffn_down_proj", "L0_ffn_down_bias"]


def kernel(**inputs):
    import concourse.bacc as bacc
    from concourse.bass_utils import run_bass_kernel_spmd

    nc = bacc.Bacc("TRN2", target_bir_lowering=False, num_devices=1)
    arrays = {f"in_{name}": np.ascontiguousarray(inputs[name]) for name in _INS}
    for name, table in zip(("cos_q", "sin_q", "cos_k", "sin_k"), rope_tables(NH, HD ** -0.5) + rope_tables(NKV, 1.0)):
        arrays[name] = table
    args = [nc.dram_tensor(name, a.shape, mybir.dt.from_np(a.dtype), kind="ExternalInput").ap() for name, a in arrays.items()]
    out = nc.dram_tensor("out", (B, S, D), F32, kind="ExternalOutput").ap()
    build(nc, *args, out)
    result = run_bass_kernel_spmd(nc, [arrays], core_ids=[0])
    return result.results[0]["out"]
```

```python
from contextlib import ExitStack

import numpy as np

import concourse.bass as bass
from concourse import mybir

ALU = mybir.AluOpType
ACT = mybir.ActivationFunctionType
F32 = mybir.dt.float32
BF16 = mybir.dt.bfloat16
F16 = mybir.dt.float16
AX_X = mybir.AxisListType.X

P = 128
B, S, D = 8, 512, 128
NH, NKV, HD = 16, 4, 8
E, TOPK, FF = 16, 4, 128
NT = S // P
NG = NH // NKV
EPS = 1e-5
ALPHA, LIMIT = 1.702, 7.0
NEG = -1.0e30
BIG = 3.0e38

Q_PART = (0, 0, 0, 1, 1, 2)
K_PART = (0, 1, 2, 0, 1, 0)
NR = len(Q_PART)
STACK = NR * HD

X_TOP, W_TOP = 4096.0, 16384.0
TINY = 1.0e-28

NU = NG * NT * 2
NV = NG * NT
NM = NG * 11
RING = 8
LAG = 4
M_FIRST = 12
M_IN_SLOT = (1, 1, 2, 1, 2, 1, 2, 1)
M_SLOT0 = 5

JOBS = {"v": ("m", 2), "oT0": ("tail", 3), "xT": ("p", 4), "oT1": ("tail", 5), "mB": ("m_prev", 8), "q": ("p", 9),
        "oT2": ("tail", 6), "qr": ("p", 10), "oT3": ("tail", 11), "k": ("p", 12), "onT": ("tail", 13), "kr": ("p", 18),
        "y": ("tail", 15), "x2": ("tail", 21), "mA": ("m", 23), "lg": ("tail", 22), "rT": ("tail", 29), "bias": ("tail", 31)}
SLOT = {name: slot for name, (_, slot) in JOBS.items()}
SLOT.update(rstd=0, xn=2, q_sum=10, q_a=12, q_left=14, q_b=15, q_c=16, k_sum=18, k_a=20, k_left=21, k_b=22, k_c=23,
            stats2=16, rstd2=17, x2n=19, x2_low=21, x2_keep=29, cut_B=5, cut_A=21, top=23, cut=25, lexp=24, wsel=26, rt=27, rt_keep=27)


def stages(n):
    return {"e": 1 <= n <= B, "e_prev": 2 <= n <= B + 1, "m": 0 <= n < B, "m_prev": 1 <= n <= B, "p": n < B - 1, "tail": n >= 2}


def jobs_of(n):
    return [name for name in sorted(JOBS, key=SLOT.get) if stages(n)[JOBS[name][0]]]


class Step:

    def __init__(self, t, par, like):
        self.t, self.par = t, par
        has = stages(like)
        self.e, self.e_prev, self.m, self.m_prev, self.p, self.tail = (has[k] for k in ("e", "e_prev", "m", "m_prev", "p", "tail"))
        self.jobs = jobs_of(like)
        before = sum(len(jobs_of(n)) for n in range(-1, min(like, 2)))
        self.before = before + len(JOBS) * (t - 2) if 2 <= like <= B - 2 else before + sum(len(jobs_of(n)) for n in range(2, like))

    def filled(self, job):
        return self.before + self.jobs.index(job) + 1

    def free(self, job):
        return self.before + self.jobs.index(job)


def m_slot(m):
    return [u for u in range(M_SLOT0, M_SLOT0 + NU) for _ in range(M_IN_SLOT[u % 8])][m]


def v_slot(n):
    return 2 * n + LAG


def m_unit(m):
    g, k = divmod(m, 11)
    if k == 0:
        return 0, NG * g, 4
    if k < 3:
        return 1, NG * g + 2 * (k - 1), 2
    return (2, NG * g + k - 3, 1) if k < 7 else (3, NG * g + k - 7, 1)


def m_units_of(st, u):
    before = [(m, st.t - 1, 1 - st.par) for m in range(NM) if m_slot(m) == u + NU and st.m_prev]
    first = M_FIRST if isinstance(st.t, int) and st.t == 0 else 0
    return before + [(m, st.t, st.par) for m in range(NM) if max(m_slot(m), first) == u and st.m]


def values_of(st, u):
    before = [(n, st.t - 2, st.par) for n in range(NV) if v_slot(n) == u + NU and st.e_prev]
    return before + [(n, st.t - 1, 1 - st.par) for n in range(NV) if v_slot(n) == u and st.e]


def build(nc, x, wq, wk, wv, wo, router_w, router_b, gate_up, gate_up_b, down, down_b, cos_q, sin_q, cos_k, sin_k, out):
    with ExitStack() as ctx:
        def sb(name, shape, dt=F32):
            return ctx.enter_context(nc.sbuf_tensor(name, shape, dt))

        def sem(name):
            return ctx.enter_context(nc.semaphore(name))

        X = sb("X", [P, B * NT, D])
        x2T = sb("x2T", [P, 2, B * S], F16)
        route = sb("route", [P, B * NT, E])
        ident = sb("ident", [P, P])
        ident_bf = sb("ident_bf", [P, P], BF16)
        mask = sb("mask", [P, 4, P], BF16)
        wq_raw, wk_raw = sb("wq_raw", [P, NH * HD]), sb("wk_raw", [P, NKV * HD])
        wq_p, wq_r = sb("wq_p", [P, HD, NH]), sb("wq_r", [P, HD, NH])
        wk_p, wk_r = sb("wk_p", [P, HD, NKV]), sb("wk_r", [P, HD, NKV])
        wv_s, wo_s = sb("wv_s", [P, NKV * HD]), sb("wo_s", [P, D])
        rw_s, rb_s = sb("rw_s", [P, E]), sb("rb_s", [P, E])
        cosq_s, sinq_s = sb("cosq_s", [P, S]), sb("sinq_s", [P, S])
        cosk_s, sink_s = sb("cosk_s", [P, P]), sb("sink_s", [P, P])
        gu_s = sb("gu_s", [P, E, 2 * FF])
        dn_s = sb("dn_s", [P, E, D])
        dnb_s = sb("dnb_s", [E, D])
        gub_s = sb("gub_s", [P, E, 2])
        gate_b, up_b = sb("gate_b", [P, E]), sb("up_b", [P, E])
        w_abs = sb("w_abs", [P, 5])
        w_max, w_inv, w_neg, w_scale = (sb(n, [P, 1]) for n in ("w_max", "w_inv", "w_neg", "w_scale"))
        ones = sb("ones", [1, P])
        mhalf, limit = sb("mhalf", [P, NT]), sb("limit", [P, 1])
        stats, mv, veps, rstd = sb("stats", [P, NT, 6]), sb("mv", [P, NT, 2]), sb("veps", [P, NT]), sb("rstd", [P, NT])
        xn, xT = sb("xn", [P, NT, D]), sb("xT", [P, S])
        rope_c, rope_s, rope, left = sb("rope_c", [P, S]), sb("rope_s", [P, S]), sb("rope", [P, S]), sb("left", [P, S])
        qparts = sb("qparts", [P, 3, S], BF16)
        kparts = sb("kparts", [P, 3, P], BF16)
        Qs = [sb(f"Qs{i}", [P, NH, S], BF16) for i in range(2)]
        Ks = [sb(f"Ks{i}", [P, NKV, S], BF16) for i in range(2)]
        Km = [sb(f"Km{i}", [P, NKV, S], BF16) for i in range(2)]
        Vs = [sb(f"Vs{i}", [P, NT, NKV, 32]) for i in range(2)]
        probs = sb("probs", [P, RING, 2, S])
        negmax = sb("negmax", [P, NT, NH])
        mcast = sb("mcast", [P, 2, NT, 2, NH // 2], BF16)
        mparts = [sb(f"mparts{i}", [NH, S], BF16) for i in range(2)]
        oT = [sb(f"oT{i}", [P, NG, S]) for i in range(2)]
        rden, on = sb("rden", [P, NT, NH]), sb("on", [P, NT, D])
        onT = sb("onT", [P, S])
        x1 = sb("x1", [P, NT, D])
        stats2, mv2, veps2, rstd2 = sb("stats2", [P, NT, 6]), sb("mv2", [P, NT, 2]), sb("veps2", [P, NT]), sb("rstd2", [P, NT])
        x2n, x2s, x2hl = sb("x2n", [P, NT, D]), sb("x2s", [P, S]), sb("x2hl", [P, 2, S], F16)
        lg, top, first4, cut = sb("lg", [P, NT, 24]), sb("top", [P, NT, 8]), sb("first4", [P, NT, 8]), sb("cut", [P, NT, 24])
        ldiff, lexp, chosen, lsum, lrec = (sb(n, [P, NT, k]) for n, k in (("ldiff", E), ("lexp", E), ("chosen", E), ("lsum", 1), ("lrec", 1)))
        wsel, rt = sb("wsel", [P, NT, E]), sb("rt", [P, NT, E])
        gu_hl = Qs[0][:].bitcast(F16).rearrange("p e (two w f) -> p e two w f", two=2, w=2)
        rtT = left[0:E, :]

        ps_e = ctx.enter_context(nc.psum_tensor("ps_e", [P, 3, S], F32))
        ps_m = ctx.enter_context(nc.psum_tensor("ps_m", [P, 3, S], F32))
        ps_o = ctx.enter_context(nc.psum_tensor("ps_o", [P, S], F32))
        ps_x = ctx.enter_context(nc.psum_tensor("ps_x", [P, S], F32))

        q_dram = nc.dram_tensor("q_dram", [2, NR, P, S], BF16, kind="Internal").ap()
        k_dram = nc.dram_tensor("k_dram", [2, NR, NKV * HD, S], BF16, kind="Internal").ap()

        x_first, x_rest, wq_in, w_in, moe_in, const_rdy = sem("x_first"), sem("x_rest"), sem("wq_in"), sem("w_in"), sem("moe_in"), sem("const_rdy")
        init, perm, zero_v, biases = sem("init"), sem("perm"), sem("zero_v"), sem("biases")
        zero_g = sem("zero_g")
        st_done, mv_done, ve_done, rs_done, xn_done = (sem(n) for n in ("st_done", "mv_done", "ve_done", "rs_done", "xn_done"))
        x_fill, x_read = sem("x_fill"), sem("x_read")
        rope_add = sem("rope_add")
        part_a, part_r, part_b, part_c = sem("part_a"), sem("part_r"), sem("part_b"), sem("part_c")
        q_spill, k_spill = sem("q_spill"), sem("k_spill")
        qs_in, km_in, ks_in = sem("qs_in"), sem("km_in"), sem("ks_in")
        mx_mm, mx_red = sem("mx_mm"), sem("mx_red")
        mh_done, ml_done, m_in = sem("mh_done"), sem("ml_done"), sem("m_in")
        sc_mm, exp_done, causal = sem("sc_mm"), sem("exp_done"), sem("causal")
        pv_mm, o_ev = sem("pv_mm"), sem("o_ev")
        rden_done = sem("rden_done")
        st2_done, mv2_done, ve2_done, rs2_done, x2n_done = (sem(n) for n in ("st2_done", "mv2_done", "ve2_done", "rs2_done", "x2n_done"))
        x2_kept, top_done, first_done, diff_done, lexp_done = (sem(n) for n in ("x2_kept", "top_done", "first_done", "diff_done", "lexp_done"))
        cut_done, chosen_done, wsel_done, lsum_done, lrec_done, rt_done, rt_kept = (
            sem(n) for n in ("cut_done", "chosen_done", "wsel_done", "lsum_done", "lrec_done", "rt_done", "rt_kept"))

        def wait(eng, s, value):
            if not isinstance(value, int) or value > 0:
                eng.wait_ge(s, value)

        def used(batch, of_batch, n):
            if n >= 3:
                return of_batch * batch + n - 2
            return of_batch * (batch - 1) + max(k for k in range(of_batch - 3, of_batch) if k % 3 == n) + 1

        oT_slots = [SLOT[f"oT{i}"] for i in range(NT)]

        def tiles(t):
            return bass.ds(t * NT, NT)

        def steps(eng, step):
            for t in (-1, 0, 1):
                step(Step(t, t % 2, t))
            with eng.Fori(2, 5, 2) as t:
                step(Step(t, 0, 2))
                step(Step(t + 1, 1, 3))
            for t in range(B - 2, B + 2):
                step(Step(t, t % 2, t))

        gate_mm, up_mm, relu_done, low_done, v_done, glu_done = (sem(n) for n in ("gate_mm", "up_mm", "relu_done", "low_done", "v_done", "glu_done"))
        act_done, down_mm, acc_done, rc_done, out_done = (sem(n) for n in ("act_done", "down_mm", "acc_done", "rc_done", "out_done"))
        max_done, flip_done, top_w, spread_done, scale_done = (sem(n) for n in ("max_done", "flip_done", "top_w", "spread_done", "scale_done"))
        high_w, low_w, x2h_done, x2l_done = sem("high_w"), sem("low_w"), sem("x2h_done"), sem("x2l_done")
        rc, acc = sb("rc", [P, NT, E]), sb("acc", [P, NT, D])
        UNITS, NB = B * E, 4
        LAST = Step(B + 1, 1, B + 1)

        def turns(eng, turn, lag):
            with eng.Fori(1, B) as c:
                for e in range(E):
                    turn(c, e)
            for n in range(lag):
                turn(B, n)

        def unit(c, e, back):
            if isinstance(c, int) and not 0 <= E * c + e - back < UNITS:
                return None
            chunk, expert = (c, e - back) if e >= back else (c - 1, e - back + E)
            return chunk, expert, E * chunk + expert

        def ps_gate(e):
            return ps_e[:, e % 2, :]

        def ps_up(e):
            return (ps_e if e % 2 else ps_m)[:, 2, :]

        def ps_down(e):
            return (ps_m[:, 0, :], ps_m[:, 1, :], ps_o[:], ps_x[:])[e]

        def down_bank(c, e):
            return e % 3 if isinstance(c, int) and c == 0 and e < E - 1 else e % NB

        def glu_s(e):
            return probs[:, e % NB, 0, :]

        def low_s(e):
            return probs[:, e % NB, 1, :]

        def act_s(e):
            return probs[:, NB + e % NB, 0, :]

        def pe_turns(pe):
            mm = nc.tensor.matmul

            def three(psum, e, which, c):
                for k, (wp, xp) in enumerate(((0, 0), (0, 1), (1, 0))):
                    last = mm(psum, gu_hl[:, e, wp, which, :], x2T[:, xp, bass.ds(c * S, S)], start=(k == 0), stop=(k == 2))
                return last

            def turn(c, e):
                if isinstance(c, int) and (c, e) == (0, 0):
                    pe.wait_ge(x2_kept, 1)
                    pe.wait_ge(low_w, NT)
                    pe.wait_ge(exp_done, 2 * NU * B)
                    pe.wait_ge(mx_red, NM * B)
                if unit(c, e, 0):
                    n = E * c + e
                    wait(pe, relu_done, n - 1)
                    three(ps_gate(e), e, 0, c).then_inc(gate_mm, 1)
                    wait(pe, low_done, n - 1)
                    three(ps_up(e), e, 1, c).then_inc(up_mm, 1)
                back = unit(c, e, 3)
                if back:
                    chunk, x, m = back
                    pe.wait_ge(act_done, m + 1)
                    if isinstance(c, int) and chunk == 0 and x == 2:
                        pe.wait_ge(o_ev, NG * B)
                    if isinstance(chunk, int) and chunk == 0 and x == E - 1:
                        pe.wait_ge(x_read, LAST.filled("bias"))
                    wait(pe, acc_done, m - (2 if isinstance(chunk, int) and chunk == 0 else NB - 1))
                    psum = ps_down(down_bank(chunk, x))
                    for i in range(NT):
                        last = mm(psum[:, D * i:D * (i + 1)], act_s(x)[:, P * i:P * (i + 1)], dn_s[:, x, :], start=True, stop=True)
                    last.then_inc(down_mm, 1)

            return turn

        def act_turns(act):
            a = nc.scalar

            def turn(c, e):
                back = unit(c, e, 1)
                if back:
                    _, x, m = back
                    act.wait_ge(relu_done, m + 1)
                    a.activation(glu_s(x), glu_s(x), ACT.Gelu_apprx_sigmoid, bias=limit[:], scale=-1.0).then_inc(glu_done, 1)
                if unit(c, e, 0):
                    n = E * c + e
                    if isinstance(c, int) and (c, e) == (0, 0):
                        act.wait_ge(const_rdy, 5)
                        act.wait_ge(biases, 2)
                        act.wait_ge(pv_mm, NV * B - 2)
                    act.wait_ge(gate_mm, n + 1)
                    wait(act, act_done, n - NB + 1)
                    a.activation(glu_s(e), ps_gate(e), ACT.Relu, bias=gate_b[:, e:e + 1], scale=w_neg[:]).then_inc(relu_done, 1)
                    act.wait_ge(up_mm, n + 1)
                    a.activation(low_s(e), ps_up(e), ACT.Relu, bias=up_b[:, e:e + 1], scale=w_neg[:]).then_inc(low_done, 1)

            return turn

        def pool_turns(pool):
            def turn(c, e):
                if unit(c, e, 0):
                    n = E * c + e
                    pool.wait_ge(low_done, n + 1)
                    pool.nop(nofuse=True)
                    nc.gpsimd.tensor_scalar(low_s(e), low_s(e), 2 * LIMIT, None, ALU.min).then_inc(v_done, 1)

            return turn

        def dve_turns(dve):
            v = nc.vector

            def turn(c, e):
                back = unit(c, e, 2)
                if back:
                    _, x, m = back
                    dve.wait_ge(glu_done, m + 1)
                    dve.wait_ge(v_done, m + 1)
                    if isinstance(c, int) and (c, x) == (0, 0):
                        dve.wait_ge(pv_mm, NV * B)
                    wait(dve, down_mm, m - NB + 1)
                    v.scalar_tensor_tensor(out=act_s(x), in0=low_s(x), scalar=LIMIT + 1.0, in1=glu_s(x),
                                           op0=ALU.subtract, op1=ALU.mult).then_inc(act_done, 1)
                back = unit(c, e, 4)
                if back:
                    chunk, x, m = back
                    if x == 0:
                        wait(dve, acc_done, m)
                        if isinstance(chunk, int):
                            dve.wait_ge(rt_kept, 1)
                        v.tensor_scalar(rc[:], route[:, tiles(chunk), :], -1.0, None, ALU.mult).then_inc(rc_done, 1)
                        dve.wait_ge(rc_done, chunk + 1)
                    dve.wait_ge(down_mm, m + 1)
                    wait(dve, acc_done, m)
                    for i in range(NT):
                        here = X[:, bass.ds(chunk * NT + i, 1), :].rearrange("p a d -> p (a d)")
                        last = v.scalar_tensor_tensor(out=here if x == E - 1 else acc[:, i, :], in0=ps_down(down_bank(chunk, x))[:, D * i:D * (i + 1)],
                                                      scalar=rc[:, i, x:x + 1], in1=here if x == 0 else acc[:, i, :],
                                                      op0=ALU.mult, op1=ALU.add)
                    last.then_inc(acc_done, 1)

            return turn

        block = ctx.enter_context(nc.Block())

        @block.sync
        def _(sp):
            sp.dma_start(X[:, 0:NT, :], x[0].rearrange("(i p) d -> p i d", p=P)).then_inc(x_first, 16)
            sp.dma_start(wq_raw[:], wq).then_inc(wq_in, 16)
            sp.dma_start(wk_raw[:], wk).then_inc(wq_in, 16)
            sp.dma_start(wv_s[:], wv).then_inc(w_in, 16)
            sp.dma_start(cosq_s[:], cos_q).then_inc(w_in, 16)
            sp.dma_start(sinq_s[:], sin_q).then_inc(w_in, 16)
            sp.dma_start(cosk_s[:], cos_k).then_inc(w_in, 16)
            sp.dma_start(sink_s[:], sin_k).then_inc(w_in, 16)
            sp.dma_start(wo_s[:], wo).then_inc(w_in, 16)
            sp.dma_start(X[:, NT:B * NT, :], x[1:B].rearrange("b (i p) d -> p (b i) d", p=P)).then_inc(x_rest, 16)
            sp.dma_start(rw_s[:], router_w).then_inc(moe_in, 16)
            sp.dma_start(rb_s[:], router_b.unsqueeze(0).to_broadcast([P, E])).then_inc(moe_in, 16)
            sp.dma_start(dnb_s[:], down_b).then_inc(moe_in, 16)
            sp.dma_start(gub_s[:], gate_up_b.rearrange("e (f two) -> f e two", two=2)).then_inc(moe_in, 16)
            sp.dma_start(gu_s[:], gate_up.rearrange("e h f -> h e f")).then_inc(moe_in, 16)
            sp.dma_start(dn_s[:], down.rearrange("e f h -> f e h")).then_inc(moe_in, 16)
            sp.wait_ge(zero_v, 9)
            sp.wait_ge(zero_g, 8)

            def spill_q(par):
                for part in range(3):
                    first, n = Q_PART.index(part), Q_PART.count(part)
                    sp.dma_start(q_dram[par, first:first + n].rearrange("r q t -> q r t"),
                                 qparts[:, part:part + 1, :].to_broadcast([P, n, S])).then_inc(q_spill, 16)

            def load_max(st, batch, par, half):
                sp.wait_ge(x_read, st.filled("mB" if half else "mA"))
                heads = slice(8 * half, 8 * half + 8)
                sp.dma_start(Qs[par][STACK:STACK + 1, heads, :], mparts[half][0:8]).then_inc(m_in, 16)
                sp.dma_start(Qs[par][STACK + 1:STACK + 2, heads, :], mparts[half][8:16]).then_inc(m_in, 16)

            def step(st):
                t, par, nxt = st.t, st.par, 1 - st.par
                if st.m_prev:
                    load_max(st, t - 1, 1 - par, 1)
                if st.p:
                    sp.wait_ge(part_c, 2 * (t + 1) + 1)
                    spill_q(nxt)
                    sp.wait_ge(part_c, 2 * (t + 1) + 2)
                    for r in range(NR):
                        sp.dma_start(k_dram[nxt, r].rearrange("q (i c) -> i q c", i=NT), kparts[:, K_PART[r], :]).then_inc(k_spill, 16)
                if st.m:
                    load_max(st, t, par, 0)
                if st.p:
                    def load_q():
                        wait(sp, sc_mm, 2 * NU * t)
                        sp.nop(nofuse=True)
                        sp.wait_ge(q_spill, 48 * (t + 2))
                        sp.dma_start(Qs[nxt][0:STACK], q_dram[nxt].rearrange("r (d h) t -> (r d) h t", d=HD)).then_inc(qs_in, 16)

                    def load_k(stack, done):
                        sp.wait_ge(k_spill, 96 * (t + 2))
                        sp.dma_start(stack[nxt][0:STACK], k_dram[nxt].rearrange("r (d h) t -> (r d) h t", d=HD)).then_inc(done, 16)

                    if isinstance(t, int) and t == -1:
                        load_q()
                        load_k(Km, km_in)
                    else:
                        wait(sp, mx_mm, NM * t)
                        load_k(Km, km_in)
                        load_q()
                    load_k(Ks, ks_in)

            steps(sp, step)
            with sp.Fori(0, B) as c:
                sp.wait_ge(acc_done, E * c + E)
                sp.dma_start(out[bass.ds(c, 1)].rearrange("a (i p) d -> p (a i) d", p=P), X[:, tiles(c), :]).then_inc(out_done, 16)
            sp.wait_ge(out_done, 16 * B)

        @block.gpsimd
        def _(pool):
            g = nc.gpsimd
            g.memset(mhalf[:], -0.5).then_inc(const_rdy, 1)
            g.memset(limit[:], LIMIT).then_inc(const_rdy, 1)
            g.memset(ones[:], 1.0).then_inc(const_rdy, 1)
            g.memset(ident[:], 0.0).then_inc(init, 1)
            g.memset(mask[:], 0.0).then_inc(init, 1)
            pool.wait_ge(init, 2)
            g.affine_select(out=ident[:], in_=ident[:], compare_op=ALU.not_equal, fill=1.0, base=0,
                            pattern=[[-1, P]], channel_multiplier=1).then_inc(init, 1)
            g.affine_select(out=mask[:], in_=mask[:], compare_op=ALU.is_ge, fill=NEG, base=0,
                            pattern=[[0, 4], [-1, P]], channel_multiplier=1).then_inc(const_rdy, 1)
            pool.wait_ge(init, 3)
            g.tensor_copy(ident_bf[:], ident[:]).then_inc(const_rdy, 1)

            def clear():
                g.memset(Qs[1][:].bitcast(F32), 0.0).then_inc(zero_g, 1)
                g.memset(Km[1][:].bitcast(F32), 0.0).then_inc(zero_g, 1)
                g.memset(Ks[1][:].bitcast(F32), 0.0).then_inc(zero_g, 1)
                g.memset(Vs[1][:], 0.0).then_inc(zero_g, 1)
                g.memset(lg[:], BIG).then_inc(zero_g, 1)
                g.memset(first4[:], BIG).then_inc(zero_g, 1)
                pool.wait_ge(zero_g, 6)
                g.memset(Vs[1][:, :, :, HD:HD + 1], 1.0).then_inc(zero_g, 1)
                pool.wait_ge(zero_g, 7)
                g.memset(Ks[1][32:64], 1.0).then_inc(zero_g, 1)
                pool.wait_ge(zero_g, 8)

            def step(st):
                t = st.t
                for u in range(NU):
                    if isinstance(t, int) and t == B + 1 and u % 2 == 0:
                        expert_turn(0, u // 2)
                    if st.e:
                        pool.wait_ge(exp_done, 2 * (NU * (t - 1) + u + 1))
                        pool.nop(nofuse=True)
                        diag = probs[:, u % RING, :, 0:P]
                        g.affine_select(out=diag, in_=diag, compare_op=ALU.is_ge, fill=0.0, base=0,
                                        pattern=[[0, 2], [1, P]], channel_multiplier=-1).then_inc(causal, 1)
                    if st.p and u == SLOT["rstd"]:
                        pool.wait_ge(ve_done, t + 2)
                        g.tensor_tensor(rstd[:], veps[:], mhalf[:], ALU.pow).then_inc(rs_done, 1)
                    if isinstance(t, int) and t == -1 and u == 2:
                        clear()
                    for part, (add, less, rest) in ((0, ("q_sum", "q_left", "q_c")), (1, ("k_sum", "k_left", "k_c"))):
                        cols, parts = (slice(0, P if part else S), kparts if part else qparts)
                        if st.p and u == SLOT[add]:
                            pool.wait_ge(x_read, st.filled("kr" if part else "qr"))
                            if part:
                                pool.wait_ge(part_c, 2 * (t + 1) + 1)
                            g.tensor_tensor(rope[:, cols], rope_c[:, cols], rope_s[:, cols], ALU.add).then_inc(rope_add, 1)
                        if st.p and u == SLOT[less]:
                            pool.wait_ge(part_a, 2 * (t + 1) + part + 1)
                            g.tensor_tensor(left[:, cols], rope[:, cols], parts[:, 0, :], ALU.subtract).then_inc(part_r, 1)
                        if st.p and u == SLOT[rest]:
                            pool.wait_ge(part_b, 2 * (t + 1) + part + 1)
                            g.tensor_tensor(parts[:, 2, :], left[:, cols], parts[:, 1, :], ALU.subtract).then_inc(part_c, 1)
                    if st.tail and u == SLOT["rstd2"]:
                        pool.wait_ge(ve2_done, t - 1)
                        g.tensor_tensor(rstd2[:], veps2[:], mhalf[:], ALU.pow).then_inc(rs2_done, 1)
                    if st.tail and u == SLOT["x2_low"]:
                        pool.wait_ge(x2h_done, t - 1)
                        g.tensor_tensor(x2hl[:, 1, :], x2s[:], x2hl[:, 0, :], ALU.subtract).then_inc(x2l_done, 1)
                    if st.tail and u == SLOT["rt_keep"]:
                        pool.wait_ge(rt_done, t - 1)
                        g.tensor_copy(route[:, tiles(t - 2), :], rt[:]).then_inc(rt_kept, 1)

            expert_turn = pool_turns(pool)
            steps(pool, step)
            turns(pool, expert_turn, 0)

        @block.tensor
        def _(pe):
            mm = nc.tensor.matmul
            pe.wait_ge(const_rdy, 5)
            pe.wait_ge(perm, 6)

            def turn(job, st, source, rows=P):
                pe.wait_ge(x_read, st.free(job))
                for i in range(NT):
                    last = nc.tensor.transpose(ps_x[0:rows, P * i:P * (i + 1)], source(i), ident[:])
                last.then_inc(x_fill, 1)

            def product(job, st, left_side, right_side, width):
                pe.wait_ge(x_read, st.free(job))
                for i in range(NT):
                    last = mm(ps_x[:, width * i:width * (i + 1)], left_side[:, P * i:P * (i + 1)], right_side[:], start=True, stop=True)
                last.then_inc(x_fill, 1)

            def project(job, st, rows, w):
                pe.wait_ge(x_read, st.free(job))
                for i in range(P // rows):
                    n = S * rows // P
                    last = mm(ps_x[rows * i:rows * (i + 1), 0:n], w[:], xT[:, n * i:n * (i + 1)], start=True, stop=True)
                last.then_inc(x_fill, 1)

            def turn_max(job, st, half):
                pe.wait_ge(x_read, st.free(job))
                for i in range(NT):
                    last = mm(ps_x[0:NH, P * i:P * (i + 1)], mcast[:, half, i].rearrange("p c h -> p (c h)"), ident_bf[:], start=True, stop=True)
                last.then_inc(x_fill, 1)

            def step(st):
                t, par = st.t, st.par
                if isinstance(t, int) and t == 1:
                    pe.wait_ge(moe_in, 16 * 6)
                for u in range(NU):
                    if isinstance(t, int) and t == B + 1 and u % 2 == 0:
                        expert_turn(0, u // 2)
                    if isinstance(t, int) and t == B and u == 14:
                        pe.wait_ge(max_done, 5)
                        pe.wait_ge(mx_red, NM * B)
                        nc.tensor.transpose(ps_m[0:1, 0, 0:P], w_abs[:, 4:5], ident[:]).then_inc(flip_done, 1)
                    if isinstance(t, int) and t == B and u == 15:
                        pe.wait_ge(top_w, 1)
                        mm(ps_m[:, 1, 0:1], ones[:], w_max[0:1, :], start=True, stop=True).then_inc(spread_done, 1)
                    for m, batch, bpar in m_units_of(st, u):
                        i, h0, nh = m_unit(m)
                        w = P * (i + 1)
                        if m == 0:
                            pe.wait_ge(km_in, 16 * (batch + 1))
                            pe.wait_ge(qs_in, 16 * (batch + 1))
                        wait(pe, mx_red, used(batch, NM, m))
                        bank = ps_m[:, m % 3, 0:nh * w].rearrange("p (h k) -> p h k", h=nh)
                        mm(bank[:, :, P * i:w], ident_bf[:], mask[:, 0:nh, :], start=True, stop=False, skip_group_check=True)
                        for k in range(nh):
                            h = h0 + k
                            last = mm(bank[:, k, :], Qs[bpar][:, h, P * i:w], Km[bpar][:, h % NKV, 0:w],
                                      start=False, stop=True, skip_group_check=True)
                        last.then_inc(mx_mm, 1)
                    if st.e:
                        g, j, pair = u // 8, u // 2 % NT, u % 2
                        if u == 0:
                            pe.wait_ge(ks_in, 16 * t)
                        if u in (0, NU // 2):
                            pe.wait_ge(m_in, 64 * (t - 1) + (32 if u == 0 else 64))
                        for k in range(2):
                            h, n = NG * g + 2 * pair + k, 2 * u + k
                            wait(pe, exp_done, used(t - 1, 2 * NU, n))
                            mm(ps_e[:, n % 3, 0:S - P * j], Ks[1 - par][:, h % NKV, P * j:P * (j + 1)],
                               Qs[1 - par][:, h, P * j:S], start=True, stop=True).then_inc(sc_mm, 1)
                    for n, batch, bpar in values_of(st, u):
                        g, j = n // NT, n % NT
                        if j == 0:
                            wait(pe, o_ev, NG * batch + g)
                        pe.wait_ge(causal, NU * batch + 2 * n + 2)
                        for k in range(4):
                            last = mm(ps_o[32 * k:32 * k + 32, P * j:S], Vs[bpar][:, j, k, :],
                                      probs[:, (2 * n + k // 2) % RING, k % 2, 0:S - P * j],
                                      start=(j == 0), stop=(j == NT - 1))
                        last.then_inc(pv_mm, 1)
                    if st.m and u == SLOT["v"]:
                        pe.wait_ge(x_read, st.free("v"))
                        for i in range(NT):
                            last = mm(ps_x[:, 32 * i:32 * i + 32], xT[:, P * i:P * (i + 1)], wv_s[:], start=True, stop=True)
                        last.then_inc(x_fill, 1)
                    if st.tail and u in oT_slots:
                        i = oT_slots.index(u)
                        pe.wait_ge(o_ev, NG * (t - 1))
                        turn(f"oT{i}", st, lambda g: oT[par][:, g, P * i:P * (i + 1)])
                    if st.p and u == SLOT["xT"]:
                        pe.wait_ge(xn_done, t + 2)
                        turn("xT", st, lambda i: xn[:, i, :])
                    if st.m_prev and u == SLOT["mB"]:
                        pe.wait_ge(ml_done, 2 * t)
                        turn_max("mB", st, 1)
                    if st.p and u == SLOT["q"]:
                        pe.wait_ge(x_read, st.filled("xT"))
                        project("q", st, P, wq_p)
                    if st.p and u == SLOT["qr"]:
                        project("qr", st, P, wq_r)
                    if st.p and u == SLOT["k"]:
                        project("k", st, 32, wk_p)
                    if st.tail and u == SLOT["onT"]:
                        pe.wait_ge(x_read, st.filled("oT3"))
                        turn("onT", st, lambda i: on[:, i, :])
                    if st.p and u == SLOT["kr"]:
                        project("kr", st, 32, wk_r)
                    if st.tail and u == SLOT["y"]:
                        pe.wait_ge(x_read, st.filled("onT"))
                        product("y", st, onT, wo_s, D)
                    if st.tail and u == SLOT["x2"]:
                        pe.wait_ge(x2n_done, t - 1)
                        turn("x2", st, lambda i: x2n[:, i, :])
                    if st.m and u == SLOT["mA"]:
                        pe.wait_ge(ml_done, 2 * t + 1)
                        turn_max("mA", st, 0)
                    if st.tail and u == SLOT["lg"]:
                        pe.wait_ge(x_read, st.filled("x2"))
                        product("lg", st, x2s, rw_s, E)
                    if st.tail and u == SLOT["rT"]:
                        pe.wait_ge(rt_done, t - 1)
                        turn("rT", st, lambda i: rt[:, i, :], rows=E)
                    if st.tail and u == SLOT["bias"]:
                        pe.wait_ge(x_read, st.filled("rT"))
                        product("bias", st, rtT, dnb_s, D)

            expert_turn = pe_turns(pe)
            steps(pe, step)
            pe.wait_ge(x2_kept, B)
            turns(pe, expert_turn, 3)

        @block.scalar
        def _(act):
            a = nc.scalar

            def step(st):
                t, par = st.t, st.par
                for u in range(NU):
                    if isinstance(t, int) and t == B + 1 and u % 2 == 0:
                        expert_turn(0, u // 2)
                    if st.e:
                        j = u // 2 % NT
                        wait(act, pv_mm, NV * (t - 1) + (u - RING) // 2 + 1)
                        for k in range(2):
                            n = 2 * u + k
                            act.wait_ge(sc_mm, 2 * NU * (t - 1) + n + 1)
                            a.activation(probs[:, u % RING, k, 0:S - P * j], ps_e[:, n % 3, 0:S - P * j], ACT.Exp).then_inc(exp_done, 1)
                    for n, batch, bpar in values_of(st, u):
                        if n % NT == NT - 1:
                            g = n // NT
                            act.wait_ge(pv_mm, NV * batch + n + 1)
                            a.activation(oT[bpar][:, g, :], ps_o[:], ACT.Copy).then_inc(o_ev, 1)
                    if st.m and u == SLOT["v"]:
                        if isinstance(t, int) and t == 0:
                            act.wait_ge(zero_v, 9)
                            act.wait_ge(zero_g, 8)
                        wait(act, pv_mm, NV * (t - 1))
                        act.wait_ge(x_fill, st.filled("v"))
                        a.activation(Vs[par][:, :, :, 0:HD], ps_x[:, 0:NT * 32].rearrange("p (i k d) -> p i k d", i=NT, d=HD),
                                     ACT.Copy).then_inc(x_read, 1)
                    if st.p and u == SLOT["xT"]:
                        act.wait_ge(x_fill, st.filled("xT"))
                        a.activation(xT[:], ps_x[:], ACT.Copy).then_inc(x_read, 1)
                    for job, slot, batch, half in (("mB", SLOT["mB"], t - 1, 1), ("mA", SLOT["mA"], t, 0)):
                        if u == slot and job in st.jobs:
                            act.wait_ge(x_fill, st.filled(job))
                            wait(act, m_in, 64 * batch + 32 * half)
                            a.activation(mparts[half][:], ps_x[0:NH], ACT.Copy).then_inc(x_read, 1)
                    if st.p and u in (SLOT["q_a"], SLOT["k_a"]):
                        w, parts, n = (S, qparts, 1) if u == SLOT["q_a"] else (P, kparts, 2)
                        wait(act, *((q_spill, 48 * (t + 1)) if u == SLOT["q_a"] else (k_spill, 96 * (t + 1))))
                        act.wait_ge(rope_add, 2 * (t + 1) + n)
                        a.activation(parts[:, 0, :], rope[:, 0:w], ACT.Copy).then_inc(part_a, 1)
                    if st.p and u in (SLOT["q_b"], SLOT["k_b"]):
                        w, parts, n = (S, qparts, 1) if u == SLOT["q_b"] else (P, kparts, 2)
                        act.wait_ge(part_r, 2 * (t + 1) + n)
                        a.activation(parts[:, 1, :], left[:, 0:w], ACT.Copy).then_inc(part_b, 1)
                    if st.tail and u == SLOT["onT"]:
                        act.wait_ge(x_fill, st.filled("onT"))
                        a.activation(onT[:], ps_x[:], ACT.Copy).then_inc(x_read, 1)
                    if st.tail and u == SLOT["x2"]:
                        act.wait_ge(x_fill, st.filled("x2"))
                        wait(act, x2_kept, t - 2)
                        a.activation(x2s[:], ps_x[:], ACT.Copy)
                        a.activation(x2hl[:, 0, :], ps_x[:], ACT.Copy).then_inc(x_read, 1)
                        act.wait_ge(x_read, st.filled("x2"))
                        act.sem_inc(x2h_done, 1)
                    if st.tail and u == SLOT["lexp"]:
                        act.wait_ge(diff_done, t - 1)
                        a.activation(lexp[:], ldiff[:], ACT.Exp).then_inc(lexp_done, 1)
                    if st.tail and u == SLOT["rT"]:
                        act.wait_ge(x_fill, st.filled("rT"))
                        a.activation(rtT[:], ps_x[0:E, :], ACT.Copy).then_inc(x_read, 1)

            expert_turn = act_turns(act)
            steps(act, step)
            turns(act, expert_turn, 1)

        @block.vector
        def _(dve):
            v = nc.vector
            dve.wait_ge(wq_in, 32)
            half = HD // 2
            for raw, plain, swapped, n in ((wq_raw, wq_p, wq_r, NH), (wk_raw, wk_p, wk_r, NKV)):
                cols = raw[:].rearrange("p (h d) -> p d h", d=HD)
                v.tensor_copy(plain[:], cols).then_inc(perm, 1)
                v.tensor_copy(swapped[:, 0:half, :], cols[:, half:HD, :]).then_inc(perm, 1)
                v.tensor_copy(swapped[:, half:HD, :], cols[:, 0:half, :]).then_inc(perm, 1)
            dve.wait_ge(x_first, 16)

            def clear(u):
                if u == SLOT["q"]:
                    dve.wait_ge(w_in, 16 * 6)
                if u in (4, 5, 8, 9):
                    k = (4, 5, 8, 9).index(u)
                    v.memset(Qs[0][:, 4 * k:4 * k + 4].bitcast(F32), 0.0).then_inc(zero_v, 1)
                if u == 10:
                    v.memset(Km[0][:].bitcast(F32), 0.0).then_inc(zero_v, 1)
                if u == 12:
                    v.memset(Ks[0][:].bitcast(F32), 0.0).then_inc(zero_v, 1)
                if u == 14:
                    v.memset(Vs[0][:], 0.0).then_inc(zero_v, 1)
                    dve.wait_ge(zero_v, 7)
                    v.memset(Vs[0][:, :, :, HD:HD + 1], 1.0).then_inc(zero_v, 1)
                    v.memset(Ks[0][32:64], 1.0).then_inc(zero_v, 1)

            def step(st):
                t, par = st.t, st.par
                if isinstance(t, int) and t == 1:
                    dve.wait_ge(moe_in, 16 * 6)
                    v.tensor_scalar(gate_b[:], gub_s[:, :, 0], -1.0, LIMIT, ALU.mult, ALU.add).then_inc(biases, 1)
                    v.tensor_scalar(up_b[:], gub_s[:, :, 1], -1.0, LIMIT, ALU.mult, ALU.add).then_inc(biases, 1)
                    dve.wait_ge(zero_g, 8)
                for u in range(NU):
                    if isinstance(t, int) and t == B + 1 and u % 2 == 0:
                        expert_turn(0, u // 2)
                    if isinstance(t, int) and t == -1:
                        clear(u)
                    for m, batch, bpar in m_units_of(st, u):
                        i, h0, nh = m_unit(m)
                        w = P * (i + 1)
                        dve.wait_ge(mx_mm, NM * batch + m + 1)
                        v.tensor_reduce(negmax[:, i, h0:h0 + nh], ps_m[:, m % 3, 0:nh * w].rearrange("p (h k) -> p h k", h=nh),
                                        AX_X, ALU.max, negate=True).then_inc(mx_red, 1)
                    if isinstance(t, int) and t == B and u in (7, 9, 11, 12):
                        k = (7, 9, 11, 12).index(u)
                        v.tensor_reduce(w_abs[:, k:k + 1], gu_s[:, 4 * k:4 * k + 4].rearrange("p e f -> p (e f)"), AX_X, ALU.max,
                                        apply_absolute_value=True).then_inc(max_done, 1)
                    if isinstance(t, int) and t == B and u == 13:
                        dve.wait_ge(max_done, 4)
                        v.tensor_reduce(w_abs[:, 4:5], w_abs[:, 0:4], AX_X, ALU.max).then_inc(max_done, 1)
                    if isinstance(t, int) and t == B and u == 14:
                        dve.wait_ge(flip_done, 1)
                        v.tensor_reduce(w_max[0:1, :], ps_m[0:1, 0, 0:P], AX_X, ALU.max).then_inc(top_w, 1)
                    if isinstance(t, int) and t == B and u == 15:
                        dve.wait_ge(spread_done, 1)
                        v.tensor_scalar(w_inv[:], ps_m[:, 1, 0:1], TINY, 1.0 / W_TOP, ALU.max, ALU.mult).then_inc(scale_done, 1)
                        dve.wait_ge(scale_done, 1)
                        v.tensor_scalar(w_neg[:], w_inv[:], -1.0 / X_TOP, None, ALU.mult).then_inc(scale_done, 1)
                        v.reciprocal(w_scale[:], w_inv[:]).then_inc(scale_done, 1)
                    if isinstance(t, int) and t == B and u in (17, 19, 21, 23):
                        q = slice(2 * (u - 17), 2 * (u - 17) + 4)
                        dve.wait_ge(scale_done, 3)
                        dve.wait_ge(sc_mm, 2 * NU * (B - 1))
                        v.tensor_scalar(gu_hl[:, q, 0], gu_s[:, q, :].rearrange("p e (f w) -> p e w f", w=2), w_scale[:], None,
                                        ALU.mult).then_inc(high_w, 1)
                    if isinstance(t, int) and t == B and u in (18, 20, 22, 24):
                        q = slice(2 * (u - 18), 2 * (u - 18) + 4)
                        dve.wait_ge(high_w, (u - 18) // 2 + 1)
                        for w in range(2):
                            last = v.scalar_tensor_tensor(out=gu_hl[:, q, 1, w, :], in0=gu_s[:, q, w:2 * FF:2], scalar=w_scale[:],
                                                          in1=gu_hl[:, q, 0, w, :], op0=ALU.mult, op1=ALU.subtract)
                        last.then_inc(low_w, 1)
                    if st.tail and u == SLOT["x2_keep"]:
                        dve.wait_ge(x2l_done, t - 1)
                        v.tensor_copy(x2T[:, :, bass.ds((t - 2) * S, S)], x2hl[:]).then_inc(x2_kept, 1)
                    if st.p and u == 0:
                        if isinstance(t, int) and t == 0:
                            dve.wait_ge(x_rest, 16)
                        for i in range(NT):
                            last = v.bn_stats(stats[:, i, :], X[:, bass.ds((t + 1) * NT + i, 1), :].rearrange("p a d -> p (a d)"))
                        last.then_inc(st_done, 1)
                        dve.wait_ge(st_done, t + 2)
                        dve.nop(nofuse=True)
                        for i in range(NT):
                            last = v.bn_aggr(mv[:, i, :], stats[:, i, :])
                        last.then_inc(mv_done, 1)
                        dve.wait_ge(mv_done, t + 2)
                        v.tensor_scalar(veps[:], mv[:, :, 1], EPS, None, ALU.add).then_inc(ve_done, 1)
                    if st.p and u == SLOT["xn"]:
                        dve.wait_ge(rs_done, t + 2)
                        for i in range(NT):
                            src = X[:, bass.ds((t + 1) * NT + i, 1), :].rearrange("p a d -> p (a d)")
                            last = v.tensor_scalar(xn[:, i, :], src, mv[:, i, 0:1], rstd[:, i:i + 1], ALU.subtract, ALU.mult)
                        last.then_inc(xn_done, 1)
                    if st.tail and u in oT_slots:
                        i = oT_slots.index(u)
                        dve.wait_ge(x_fill, st.filled(f"oT{i}"))
                        heads = ps_x[:].rearrange("p (h w) -> p h w", w=32)
                        v.reciprocal(rden[:, i, :], heads[:, :, HD]).then_inc(rden_done, 1)
                        dve.wait_ge(rden_done, NT * (t - 2) + i + 1)
                        v.tensor_tensor(on[:, i, :].rearrange("p (h d) -> p h d", d=HD), heads[:, :, 0:HD],
                                        rden[:, i, :].unsqueeze(2).to_broadcast([P, NH, HD]), ALU.mult).then_inc(x_read, 1)
                    for exists, slot, batch, half in ((st.m_prev, SLOT["cut_B"], t - 1, 1), (st.m, SLOT["cut_A"], t, 0)):
                        if u == slot and exists:
                            dve.wait_ge(mx_red, NM * batch + NM // 2 * (half + 1))
                            exact = negmax[:, :, 8 * half:8 * half + 8]
                            v.tensor_copy(mcast[:, half, :, 0, :], exact).then_inc(mh_done, 1)
                            dve.wait_ge(mh_done, 2 * batch + half + 1)
                            v.tensor_tensor(mcast[:, half, :, 1, :], exact, mcast[:, half, :, 0, :], ALU.subtract).then_inc(ml_done, 1)
                    if st.p and u in (SLOT["q"], SLOT["qr"], SLOT["k"], SLOT["kr"]):
                        job, w, table, to = {SLOT["q"]: ("q", S, cosq_s, rope_c), SLOT["qr"]: ("qr", S, sinq_s, rope_s),
                                             SLOT["k"]: ("k", P, cosk_s, rope_c), SLOT["kr"]: ("kr", P, sink_s, rope_s)}[u]
                        if u == SLOT["k"]:
                            dve.wait_ge(rope_add, 2 * (t + 1) + 1)
                        dve.wait_ge(x_fill, st.filled(job))
                        v.tensor_tensor(to[:, 0:w], ps_x[:, 0:w], table[:], ALU.mult).then_inc(x_read, 1)
                    if st.tail and u == SLOT["y"]:
                        dve.wait_ge(x_fill, st.filled("y"))
                        v.tensor_tensor(x1[:], X[:, tiles(t - 2), :], ps_x[:].rearrange("p (i d) -> p i d", d=D), ALU.add).then_inc(x_read, 1)
                    if st.tail and u == SLOT["stats2"]:
                        dve.wait_ge(x_read, st.filled("y"))
                        for i in range(NT):
                            last = v.bn_stats(stats2[:, i, :], x1[:, i, :])
                        last.then_inc(st2_done, 1)
                        dve.wait_ge(st2_done, t - 1)
                        dve.nop(nofuse=True)
                        for i in range(NT):
                            last = v.bn_aggr(mv2[:, i, :], stats2[:, i, :])
                        last.then_inc(mv2_done, 1)
                        dve.wait_ge(mv2_done, t - 1)
                        v.tensor_scalar(veps2[:], mv2[:, :, 1], EPS, X_TOP ** -2, ALU.add, ALU.mult).then_inc(ve2_done, 1)
                    if st.tail and u == SLOT["x2n"]:
                        dve.wait_ge(rs2_done, t - 1)
                        for i in range(NT):
                            last = v.tensor_scalar(x2n[:, i, :], x1[:, i, :], mv2[:, i, 0:1], rstd2[:, i:i + 1], ALU.subtract, ALU.mult)
                        last.then_inc(x2n_done, 1)
                    if st.tail and u == SLOT["lg"]:
                        dve.wait_ge(x_fill, st.filled("lg"))
                        v.scalar_tensor_tensor(out=lg[:, :, 0:E], in0=ps_x[:, 0:NT * E].rearrange("p (i e) -> p i e", e=E),
                                               scalar=1.0 / X_TOP, in1=rb_s[:].unsqueeze(1).to_broadcast([P, NT, E]),
                                               op0=ALU.mult, op1=ALU.add).then_inc(x_read, 1)
                    if st.tail and u == SLOT["top"]:
                        dve.wait_ge(x_read, st.filled("lg"))
                        dve.nop(nofuse=True)
                        for i in range(NT):
                            last = v.max(top[:, i, :], lg[:, i, 0:E])
                        last.then_inc(top_done, 1)
                        dve.wait_ge(top_done, t - 1)
                        v.tensor_tensor(ldiff[:], lg[:, :, 0:E], top[:, :, 0:1].to_broadcast([P, NT, E]), ALU.subtract).then_inc(diff_done, 1)
                        v.tensor_copy(first4[:, :, 0:TOPK], top[:, :, 0:TOPK]).then_inc(first_done, 1)
                    if st.tail and u == SLOT["cut"]:
                        dve.wait_ge(first_done, t - 1)
                        dve.nop(nofuse=True)
                        for i in range(NT):
                            last = v.match_replace(cut[:, i, :], first4[:, i, :], lg[:, i, :], -BIG)
                        last.then_inc(cut_done, 1)
                        dve.wait_ge(cut_done, t - 1)
                        v.tensor_tensor(chosen[:], cut[:, :, 0:E], lg[:, :, 0:E], ALU.not_equal).then_inc(chosen_done, 1)
                    if st.tail and u == SLOT["wsel"]:
                        dve.wait_ge(chosen_done, t - 1)
                        dve.wait_ge(lexp_done, t - 1)
                        v.tensor_tensor(wsel[:], lexp[:], chosen[:], ALU.mult).then_inc(wsel_done, 1)
                        dve.wait_ge(wsel_done, t - 1)
                        v.tensor_reduce(lsum[:], wsel[:], AX_X, ALU.add).then_inc(lsum_done, 1)
                    if st.tail and u == SLOT["rt"]:
                        dve.wait_ge(lsum_done, t - 1)
                        v.reciprocal(lrec[:], lsum[:]).then_inc(lrec_done, 1)
                        dve.wait_ge(lrec_done, t - 1)
                        wait(dve, rt_kept, t - 2)
                        v.tensor_tensor(rt[:], wsel[:], lrec[:].to_broadcast([P, NT, E]), ALU.mult).then_inc(rt_done, 1)
                    if st.tail and u == SLOT["bias"]:
                        dve.wait_ge(x_fill, st.filled("bias"))
                        v.tensor_tensor(X[:, tiles(t - 2), :], x1[:], ps_x[:].rearrange("p (i d) -> p i d", d=D), ALU.add).then_inc(x_read, 1)

            expert_turn = dve_turns(dve)
            steps(dve, step)
            dve.wait_ge(rt_kept, B)
            turns(dve, expert_turn, 4)


def rope_tables(heads, scale):
    half = HD // 2
    freq = (np.float32(1.0) / np.float32(10000.0) ** (np.arange(half, dtype=np.float32) / np.float32(half))).astype(np.float32)
    ang = np.arange(S, dtype=np.float32)[:, None] * freq[None, :]
    cos = np.concatenate([np.cos(ang), np.cos(ang)], 1).T * np.float32(scale)
    sin = np.concatenate([-np.sin(ang), np.sin(ang)], 1).T * np.float32(scale)
    rows = [np.repeat(t, heads, 0) for t in (cos, sin)]
    pieces = P // (heads * HD)
    return tuple(np.ascontiguousarray(np.concatenate(np.split(t, pieces, 1), 0), dtype=np.float32) for t in rows)


_INS = ["L0_attn_x", "L0_attn_wq", "L0_attn_wk", "L0_attn_wv", "L0_attn_wo", "L0_ffn_router_w", "L0_ffn_router_b",
        "L0_ffn_gate_up_proj", "L0_ffn_gate_up_bias", "L0_ffn_down_proj", "L0_ffn_down_bias"]


def kernel(**inputs):
    import concourse.bacc as bacc
    from concourse.bass_utils import run_bass_kernel_spmd

    nc = bacc.Bacc("TRN2", target_bir_lowering=False, num_devices=1)
    arrays = {f"in_{name}": np.ascontiguousarray(inputs[name]) for name in _INS}
    for name, table in zip(("cos_q", "sin_q", "cos_k", "sin_k"), rope_tables(NH, HD ** -0.5) + rope_tables(NKV, 1.0)):
        arrays[name] = table
    args = [nc.dram_tensor(name, a.shape, mybir.dt.from_np(a.dtype), kind="ExternalInput").ap() for name, a in arrays.items()]
    out = nc.dram_tensor("out", (B, S, D), F32, kind="ExternalOutput").ap()
    build(nc, *args, out)
    result = run_bass_kernel_spmd(nc, [arrays], core_ids=[0])
    return result.results[0]["out"]
```
